# Optimizing a Trainium2 kernel written in Bass

```python
import numpy as np
import jax
import jax.numpy as jnp

def _softmax(x, axis=-1):
    return jax.nn.softmax(x, axis=axis)

def _gelu(x):
    return jax.nn.gelu(x, approximate=True)

def _silu(x):
    return jax.nn.silu(x)

def _sigmoid(x):
    return jax.nn.sigmoid(x)

def _layernorm(x, axis=-1, eps=1e-05):
    m = jnp.mean(x, axis=axis, keepdims=True)
    v = jnp.var(x, axis=axis, keepdims=True)
    return (x - m) / jnp.sqrt(v + eps)

def _scatter_add(tgt, idx, src, axis=0):
    return tgt.at[idx].add(src)

def _segment_sum(src, seg, n):
    return jax.ops.segment_sum(src, seg, n)
kernel_name = 'mk_adaln_ffn_d2_seqx_r8_1b1389'

def setup_inputs(seed: int=0):
    np.random.seed(seed)
    _w = jnp.asarray

    def _rec_inputs():
        import jax
        import jax.numpy as jnp
        _rk = jax.random.key(seed)
        x = -0.0003929 + 0.9999 * jax.random.normal(jax.random.fold_in(_rk, 1), (64, 32, 512), jnp.float32)
        _lenS = 32 - jax.random.randint(jax.random.fold_in(_rk, 7), (64,), 0, max(1, 32 // 4) + 1, jnp.int32)
        _lenS2 = 32 - jax.random.randint(jax.random.fold_in(_rk, 8), (64,), 0, max(1, 32 // 4) + 1, jnp.int32)
        itok_B_8_3872 = jax.random.randint(jax.random.fold_in(_rk, 11), (64,), 8, 3873, jnp.int32)
        itok_B_3_7 = jax.random.randint(jax.random.fold_in(_rk, 12), (64,), 3, 8, jnp.int32)
        return (x, itok_B_8_3872, itok_B_3_7)
    x, itok_B_8_3872, itok_B_3_7 = _rec_inputs()

    def _L0_cond_setup():
        import math
        import jax, jax.numpy as jnp
        import numpy as np
        H, N, B, L = (32, 64, 16, 512)
        DT_MIN, DT_MAX = (0.001, 0.1)

        def _get_kernel(log_dt, C, log_A_real, A_imag, length):
            Cc = C[..., 0] + 1j * C[..., 1]
            dt = jnp.exp(log_dt)
            A = -jnp.exp(log_A_real) + 1j * A_imag
            dtA = A * dt[:, None]
            P = dtA[:, :, None] * jnp.arange(length, dtype=jnp.float32)
            Cs = Cc * (jnp.exp(dtA) - 1.0) / A
            K = 2.0 * jnp.einsum('hn,hnl->hl', Cs, jnp.exp(P)).real
            return K
        key = jax.random.key(seed)
        ks = jax.random.split(key, 6)
        u = jax.random.normal(ks[0], (B, H, L), dtype=jnp.float32)
        length = jax.random.randint(ks[1], (B,), 0, L)
        log_dt = jax.random.uniform(ks[2], (H,), dtype=jnp.float32) * (math.log(DT_MAX) - math.log(DT_MIN)) + math.log(DT_MIN)
        C = jax.random.normal(ks[3], (H, N, 2), dtype=jnp.float32)
        log_A_real = jnp.log(0.5 * jnp.ones((H, N), dtype=jnp.float32))
        A_imag = math.pi * jnp.broadcast_to(jnp.arange(N, dtype=jnp.float32), (H, N))
        D = jax.random.normal(ks[4], (H,), dtype=jnp.float32)
        return {'u': u, 'length': length, 'log_dt': log_dt, 'C': C, 'log_A_real': log_A_real, 'A_imag': A_imag, 'D': D}
    _L0_cond_all = _L0_cond_setup()
    _L0_cond_in = {k: v for k, v in _L0_cond_all.items() if k in ('log_dt', 'C', 'log_A_real', 'A_imag', 'D')}
    del _L0_cond_all

    def _L0_ffn_setup():
        import jax, jax.numpy as jnp
        import numpy as np
        D_MODEL = 512
        D_FF = 1376
        key = jax.random.key(seed)
        k1, k2, k3, k4 = jax.random.split(key, 4)
        x = jax.random.normal(k1, (2, 256, D_MODEL), dtype=jnp.float32)
        W_gate = jax.random.normal(k2, (D_FF, D_MODEL), dtype=jnp.float32) * D_MODEL ** (-0.5)
        W_up = jax.random.normal(k3, (D_FF, D_MODEL), dtype=jnp.float32) * D_MODEL ** (-0.5)
        W_down = jax.random.normal(k4, (D_MODEL, D_FF), dtype=jnp.float32) * D_FF ** (-0.5)
        return {'x': x, 'W_gate': W_gate, 'W_up': W_up, 'W_down': W_down}
    _L0_ffn_all = _L0_ffn_setup()
    _L0_ffn_in = {k: v for k, v in _L0_ffn_all.items() if k in ('W_gate', 'W_up', 'W_down')}
    del _L0_ffn_all

    def _L1_cond_setup():
        import jax, jax.numpy as jnp
        import numpy as np
        MAX_LORAS, OUT, IN = (8, 512, 512)
        B, S = (4, 256)
        key = jax.random.key(seed)
        k1, k2, k3 = jax.random.split(key, 3)
        x = jax.random.normal(k1, (B, S, IN), dtype=jnp.float32)
        weight = jax.random.normal(k2, (MAX_LORAS, OUT, IN), dtype=jnp.float32) * 0.02
        adapter_ids = jax.random.randint(k3, (B,), 0, MAX_LORAS, dtype=jnp.int32)
        return {'x': x, 'weight': weight, 'adapter_ids': adapter_ids}
    _L1_cond_all = _L1_cond_setup()
    _L1_cond_in = {k: v for k, v in _L1_cond_all.items() if k in ('weight',)}
    del _L1_cond_all

    def _L1_ffn_setup():
        import jax, jax.numpy as jnp
        import numpy as np
        R = 16
        LORA_ALPHA = 16
        SCALING = LORA_ALPHA / R
        key = jax.random.key(seed)
        kx, kr, ka = jax.random.split(key, 3)
        B, S, D, DO, E = (4, 256, 512, 512, 8)
        x = jax.random.normal(kx, (B, S, D), dtype=jnp.float32)
        bound_r = 1.0 / np.sqrt(D)
        route_w = jax.random.uniform(kr, (E, D), jnp.float32, -bound_r, bound_r)
        bound_a = 1.0 / np.sqrt(D)
        A = jax.random.uniform(ka, (E, R, D), jnp.float32, -bound_a, bound_a)
        kb = jax.random.fold_in(key, 7)
        Bw = jax.random.normal(kb, (E, DO, R), dtype=jnp.float32) * 0.02
        return {'x': x, 'route_w': route_w, 'A': A, 'Bw': Bw}
    _L1_ffn_all = _L1_ffn_setup()
    _L1_ffn_in = {k: v for k, v in _L1_ffn_all.items() if k in ('route_w', 'A', 'Bw')}
    del _L1_ffn_all
    return {'x': x, 'itok_B_8_3872': itok_B_8_3872, 'itok_B_3_7': itok_B_3_7, 'L0_cond_log_dt': _L0_cond_in['log_dt'], 'L0_cond_C': _L0_cond_in['C'], 'L0_cond_log_A_real': _L0_cond_in['log_A_real'], 'L0_cond_A_imag': _L0_cond_in['A_imag'], 'L0_cond_D': _L0_cond_in['D'], 'L0_ffn_W_gate': _L0_ffn_in['W_gate'], 'L0_ffn_W_up': _L0_ffn_in['W_up'], 'L0_ffn_W_down': _L0_ffn_in['W_down'], 'L1_cond_weight': _L1_cond_in['weight'], 'L1_ffn_route_w': _L1_ffn_in['route_w'], 'L1_ffn_A': _L1_ffn_in['A'], 'L1_ffn_Bw': _L1_ffn_in['Bw']}

def reference(x, itok_B_8_3872, itok_B_3_7, L0_cond_log_dt, L0_cond_C, L0_cond_log_A_real, L0_cond_A_imag, L0_cond_D, L0_ffn_W_gate, L0_ffn_W_up, L0_ffn_W_down, L1_cond_weight, L1_ffn_route_w, L1_ffn_A, L1_ffn_Bw):
    import jax
    import jax.numpy as jnp

    def _L0_cond_ref(u, length, log_dt, C, log_A_real, A_imag, D):
        import math
        import jax, jax.numpy as jnp
        import numpy as np
        H, N, B, L = (32, 64, 16, 512)
        DT_MIN, DT_MAX = (0.001, 0.1)

        def _get_kernel(log_dt, C, log_A_real, A_imag, length):
            Cc = C[..., 0] + 1j * C[..., 1]
            dt = jnp.exp(log_dt)
            A = -jnp.exp(log_A_real) + 1j * A_imag
            dtA = A * dt[:, None]
            P = dtA[:, :, None] * jnp.arange(length, dtype=jnp.float32)
            Cs = Cc * (jnp.exp(dtA) - 1.0) / A
            K = 2.0 * jnp.einsum('hn,hnl->hl', Cs, jnp.exp(P)).real
            return K
        Bq, Hq, Lq = u.shape
        mask = (jnp.arange(Lq) < length[:, None]).astype(u.dtype)
        u_m = u * mask[:, None, :]
        kernel = _get_kernel(log_dt, C, log_A_real, A_imag, Lq)
        n = 2 * Lq
        k_f = jnp.fft.rfft(kernel, n=n)
        u_f = jnp.fft.rfft(u_m, n=n)
        y = jnp.fft.irfft(u_f * k_f, n=n)[..., :Lq]
        y = y + u_m * D[:, None]
        return y * mask[:, None, :]

    def _L0_ffn_ref(x, W_gate, W_up, W_down):
        import jax, jax.numpy as jnp
        import numpy as np
        D_MODEL = 512
        D_FF = 1376
        out_shape = x.shape[:-1] + (W_down.shape[0],)
        xf = x.reshape(-1, x.shape[-1])
        up = jnp.einsum('td,fd->tf', xf, W_up)
        gate = jax.nn.silu(jnp.einsum('td,fd->tf', xf, W_gate))
        h = gate * up
        y = jnp.einsum('tf,df->td', h, W_down)
        return y.reshape(out_shape)

    def _L1_cond_ref(x, weight, adapter_ids):
        import jax, jax.numpy as jnp
        import numpy as np
        MAX_LORAS, OUT, IN = (8, 512, 512)
        B, S = (4, 256)
        w = weight[adapter_ids]
        return jnp.einsum('bsi,boi->bso', x, w)

    def _L1_ffn_ref(x, route_w, A, Bw):
        import jax, jax.numpy as jnp
        import numpy as np
        R = 16
        LORA_ALPHA = 16
        SCALING = LORA_ALPHA / R
        logits = jnp.einsum('bsd,ed->bse', x, route_w)
        topk_v, topk_idx = jax.lax.top_k(logits, 1)
        E = logits.shape[-1]
        route_weight = jax.nn.one_hot(topk_idx[..., 0], E, dtype=logits.dtype) * topk_v
        h = jnp.einsum('bsd,erd->bser', x, A)
        wh = route_weight[..., None] * h
        out = jnp.einsum('bser,eor->bso', wh, Bw) * SCALING
        return out
    x = x + _L0_ffn_ref(_L0_cond_ref(x, itok_B_8_3872, L0_cond_log_dt, L0_cond_C, L0_cond_log_A_real, L0_cond_A_imag, L0_cond_D), L0_ffn_W_gate, L0_ffn_W_up, L0_ffn_W_down)
    x = x + _L1_ffn_ref(_L1_cond_ref(x, L1_cond_weight, itok_B_3_7), L1_ffn_route_w, L1_ffn_A, L1_ffn_Bw)
    return x

_drawn_inputs = setup_inputs


def setup_inputs(seed=0):
    import zlib

    import numpy as np

    out = dict(_drawn_inputs(seed))
    spreads = {'L0_cond_log_A_real': (-0.6931471824645996, 0.2)}
    factors = {}
    for name, (base, spread) in spreads.items():
        noise = np.random.default_rng([zlib.crc32(name.encode()), seed]).standard_normal(out[name].shape)
        drawn = base * np.exp(spread * noise) if base else spread * noise
        out[name] = jnp.asarray(drawn.astype(out[name].dtype))
    for name, factor in factors.items():
        out[name] = (out[name] * factor).astype(out[name].dtype)
    return out
```

```python
from contextlib import ExitStack

import concourse.bass as bass
from concourse import mybir

ALU = mybir.AluOpType
ACT = mybir.ActivationFunctionType
F32 = mybir.dt.float32
F32R = mybir.dt.float32r
I32 = mybir.dt.int32
AX_X = mybir.AxisListType.X

P = 128
B, H, L = 64, 32, 512
N_STATE = 64
D_FF = 1376
E, R = 8, 16
C = L // P
F = -(-D_FF // P)
ER = E * R
Z = E + ER
NA = 16
NB = L // NA
TOK = B * H
TILE = 512
NT = TOK // TILE
BT = TILE // H
G = TILE // P
GB = P // H
PAIRS = H // 2
KROW = P + L

K_ID, K_A, K_B, K_L, K_SIGN, K_OFF, K_RANK, K_END = 0, 128, 144, 176, 180, 181, 182, 190

LOG2E = 1.4426950408889634
LN2_HI = 0.693359375
LN2_LO = -2.12194440054690583e-4
ROUND = 12582912.0
INV_2PI = 0.15915494309189535
TWO_PI = 6.283185


def build(nc, params, consts, d_skip, lens, ids, ut, xn, wgu, wd, we, ra, b2, out):
    ctx = ExitStack()
    with ctx:
        at = [16512]

        def sb(name, shape, dt, off=None):
            size = 4
            for n in shape[1:]:
                size *= n
            if off is None:
                off, at[0] = at[0], at[0] + -(-size // 32) * 32
            return nc.alloc_sbuf_tensor_at(name, shape, dt, offset=off)

        def region(size):
            off, at[0] = at[0], at[0] + size
            return off

        def sem(name):
            return ctx.enter_context(nc.semaphore(name))

        def ps(name):
            return ctx.enter_context(nc.psum_tensor(name, [P, 512], F32))

        r_whi, r_wlo = region(F * 4096), region(F * 4096)
        r_wd, r_uy, r_y = region(F * 2048), region(H * 1024), region(16384)
        r_h, r_wds, r_gt = region(8192), region(8192), region(4096)
        r_x1, r_mb = region(8192), region(GB * C * Z * 4)
        r_xn = region(4096 + 2048 + 512 + 512)
        w_hi = sb("w_hi", [P, F, 2, C, P], F32R, r_whi)
        w_lo = sb("w_lo", [P, F, 2, C, P], F32R, r_wlo)
        wd_raw = sb("wd_raw", [P, F, L], F32, r_wd)
        uy = sb("uy", [P, H, C, B], F32, r_uy)
        y_hi = sb("y_hi", [P, C, TILE], F32R, r_y)
        y_lo = sb("y_lo", [P, C, TILE], F32R, r_y + 8192)
        h_hi = sb("h_hi", [P, 2, TILE], F32R, r_h)
        h_lo = sb("h_lo", [P, 2, TILE], F32R, r_h + 4096)
        wd_hi = sb("wd_hi", [P, 2, L], F32R, r_wds)
        wd_lo = sb("wd_lo", [P, 2, L], F32R, r_wds + 4096)
        gate_sb = sb("gate_sb", [P, TILE], F32, r_gt)
        prod_sb = sb("prod_sb", [P, TILE], F32, r_gt + 2048)
        x1 = sb("x1", [P, G, L], F32, r_x1)
        mb = sb("mb", [P, GB, C, Z], F32, r_mb)
        xn_sb = sb("xn_sb", [P, 2, L], F32, r_xn)
        x1t = sb("x1t", [P, C, P], F32, r_xn + 4096)
        wh = sb("wh", [P, ER], F32, r_xn + 6144)
        wht = sb("wht", [P, P], F32, r_xn + 6656)
        b2_sb = sb("b2_sb", [P, L], F32)
        con = sb("con", [P, K_END], F32)
        mask = sb("mask", [P, C, B], F32)
        len_sb = sb("len_sb", [P, B], I32)
        id_sb = sb("id_sb", [1, B], I32)
        id_neg = sb("id_neg", [1, B], F32)
        id_fit = sb("id_fit", [1, B], F32)
        id_row = sb("id_row", [1, B], I32)
        mx = sb("mx", [P, 1], F32)
        cand = sb("cand", [P, E], F32)
        first = sb("first", [P, 1], F32)
        rw = sb("rw", [P, E], F32)
        dk_sb = sb("dk_sb", [1, H], F32)
        toep = sb("toep", [P, 4, 2, L], F32, r_y)
        we_sb = sb("we_sb", [P, 4, C, L], F32, r_wlo + 3 * 4096)
        stage = sb("stage", [P, 4, 2 * C * P], F32, r_x1)
        aw_sb = sb("aw_sb", [P, 2, C, Z], F32, r_xn)
        ra_sb = sb("ra_sb", [P, C, Z], F32, r_xn + 4352)
        phase = sb("phase", [P, 2048], F32, r_wd)
        whole = sb("whole", [P, 2048], F32, r_wd + 8192)
        expo = sb("expo", [P, 1536], F32, r_wd + 16384)
        u_tab = sb("u_tab", [P, H, NA], F32, r_h)
        v_tab = sb("v_tab", [P, H, NB], F32, r_h + 2048)
        q_tab = sb("q_tab", [P, H, NA], F32, r_h + 6144)
        k_sb = sb("k_sb", [NA, H, NB], F32, r_gt)
        par = sb("par", [P, 5, H], F32, r_wds)
        small = sb("small", [P, 40, H], F32, r_wds + 640)
        assert at[0] <= nc.sbuf_top
        zero = sb("zero", [H, P], F32, r_mb + GB * C * Z * 4 - 512)
        ident = con[:, K_ID:K_ID + P]

        gate_ps, up_ps = ps("gate_ps"), ps("up_ps")
        down_ps = [ps(f"down_ps{g}") for g in range(G)]
        s_ps, z_ps = ps("s_ps"), ps("z_ps")
        aw_ps = [[gate_ps, up_ps], [s_ps, z_ps]]
        k_ps = down_ps[0:2]

        k_dram = nc.dram_tensor("k_dram", [H, KROW], F32)
        aw_dram = nc.dram_tensor("aw_dram", [P, E * C * Z], F32)

        par_in, con_in, ra_in, b2_in, wd_in = sem("par_in"), sem("con_in"), sem("ra_in"), sem("b2_in"), sem("wd_in")
        we_in = [sem(f"we_in{i}") for i in range(4)]
        ut_in = [sem(f"ut_in{i}") for i in range(4)]
        toep_in = [sem(f"toep_in{i}") for i in range(4)]
        stage_in = [sem(f"stage_in{i}") for i in range(4)]
        xn_in = [sem(f"xn_in{i}") for i in range(2)]
        mb_in = [sem(f"mb_in{i}") for i in range(GB)]
        out_done = [sem(f"out_done{g}") for g in range(G)]
        k_out, aw_out = sem("k_out"), [sem(f"aw_out{i}") for i in range(2)]
        s4, sin_done, exp_done, tab_done = sem("s4"), sem("sin_done"), sem("exp_done"), sem("tab_done")
        k_done, k_ready, mask_done, ids_done = sem("k_done"), sem("k_ready"), sem("mask_done"), sem("ids_done")
        aw_done, aw_copied = sem("aw_done"), sem("aw_copied")
        conv_done, y_done = sem("conv_done"), sem("y_done")
        whi_done, wlo_done = sem("whi_done"), sem("wlo_done")
        yhi_done, ylo_done = sem("yhi_done"), sem("ylo_done")
        gate_done, up_done, down_done = sem("gate_done"), sem("up_done"), sem("down_done")
        silu_done, prod_done = sem("silu_done"), sem("prod_done")
        hhi_done, hlo_done, wdhi_done, wdlo_done = sem("hhi_done"), sem("hlo_done"), sem("wdhi_done"), sem("wdlo_done")
        x1_done, x1t_ps, x1t_done = sem("x1_done"), sem("x1t_ps"), sem("x1t_done")
        z_done, wh_done, wht_ps, wht_done = sem("z_done"), sem("wh_done"), sem("wht_ps"), sem("wht_done")
        o_done, out_ready, route = sem("o_done"), sem("out_ready"), sem("route")

        SLOTS = 2 * G + 2

        block = ctx.enter_context(nc.Block())

        @block.sync
        def _(sp):
            sp.dma_start(par[:, :, :], params).then_inc(par_in, 16)
            sp.dma_start(con[:, :], consts).then_inc(con_in, 16)
            sp.dma_start(dk_sb[:, :], d_skip).then_inc(con_in, 16)
            sp.dma_start(len_sb[:, :], lens).then_inc(con_in, 16)
            sp.dma_start(id_sb[:, :], ids).then_inc(con_in, 16)
            sp.dma_start(ra_sb[:, :, :], ra).then_inc(ra_in, 16)
            for s in range(4):
                sp.dma_start(we_sb[:, s, :, :], we[s]).then_inc(we_in[s], 16)
            for q in range(4):
                sp.dma_start(uy[:, 8 * q:8 * q + 8, :, :], ut[:, 8 * q:8 * q + 8]).then_inc(ut_in[q], 16)
            sp.wait_ge(aw_done, 1)
            sp.dma_start(we_sb[:, 0, :, :], we[4]).then_inc(we_in[0], 16)
            sp.wait_ge(aw_done, 2)
            sp.dma_start(we_sb[:, 1, :, :], we[5]).then_inc(we_in[1], 16)
            sp.wait_ge(aw_done, 3)
            sp.dma_start(we_sb[:, 2, :, :], we[6]).then_inc(we_in[2], 16)
            sp.wait_ge(aw_done, 4)
            sp.dma_start(we_sb[:, 3, :, :], we[7]).then_inc(we_in[3], 16)
            sp.dma_start(b2_sb[:, :], b2).then_inc(b2_in, 16)
            for f in range(2):
                sp.dma_start(stage[:, f, :], wgu[f]).then_inc(stage_in[f], 16)
            sp.wait_ge(k_ready, 2)
            sp.dma_start(k_dram[:, 0:P], zero[:, :]).then_inc(k_out, 16)
            sp.dma_start(k_dram[:, P:KROW].rearrange("h (a b) -> a h b", a=NA), k_sb[:, :, :]).then_inc(k_out, 16)
            sp.wait_ge(k_out, 32)
            def toep_src(pair):
                return bass.AP(k_dram, pair * 2 * KROW + 1, [[1, P], [KROW, 2], [1, L]])

            for s in range(4):
                sp.dma_start(toep[:, s, :, :], toep_src(s)).then_inc(toep_in[s], 16)
            with sp.Fori(1, PAIRS // 4) as i:
                for s in range(4):
                    sp.wait_ge(conv_done, i * 4 + (s - 3))
                    sp.dma_start(toep[:, s, :, :], toep_src(i * 4 + s)).then_inc(toep_in[s], 16)
            for f in range(2, 4):
                sp.dma_start(stage[:, f, :], wgu[f]).then_inc(stage_in[f], 16)
            sp.dma_start(wd_raw[:, :, :], wd).then_inc(wd_in, 16)
            for f in range(4, F):
                sp.wait_ge(whi_done, f - 3)
                sp.wait_ge(wlo_done, f - 3)
                sp.dma_start(stage[:, f % 4, :], wgu[f]).then_inc(stage_in[f % 4], 16)
            sp.wait_ge(aw_out[0], 16 * (E // 2))
            sp.wait_ge(aw_out[1], 16 * (E // 2))
            for n in range(2):
                sp.dma_start(xn_sb[:, n, :], xn[n]).then_inc(xn_in[n], 16)

            def load_x(n, slot):
                sp.wait_ge(x1_done, n - 1)
                sp.dma_start(xn_sb[:, slot, :], xn[bass.ds(n, 1)].rearrange("o p d -> p (o d)")).then_inc(xn_in[slot], 16)

            def store(n, g):
                sp.wait_ge(out_ready, n + 1)
                sp.dma_start(out[bass.ds(n, 1)].rearrange("o p d -> p (o d)"), x1[:, g, :]).then_inc(out_done[g], 16)

            with sp.Fori(0, NT - 1) as t:
                for k in range(G):
                    load_x(t * G + (k + 2), k % 2)
                for g in range(G):
                    store(t * G + g, g)
            for k in range(2):
                load_x((NT - 1) * G + k + 2, k)
            for g in range(G):
                store((NT - 1) * G + g, g)
            for g in range(G):
                sp.wait_ge(out_done[g], 16 * NT)

        @block.gpsimd
        def _(pool):
            pool.wait_ge(ids_done, 1)
            pool.wait_ge(wlo_done, F)
            pool.wait_ge(whi_done, F)
            pool.wait_ge(aw_out[0], 16 * (E // 2))
            pool.wait_ge(aw_out[1], 16 * (E // 2))

            def gather(b, j):
                e = pool.value_load(id_row[0:1, bass.ds(b, 1)], min_val=0, max_val=E - 1)
                pool.dma_start(mb[:, j, :, :], aw_dram[:, bass.ds(e * (C * Z), C * Z)]
                               .rearrange("p (c z) -> p c z", c=C)).then_inc(mb_in[j], 16)

            for j in range(GB):
                gather(j, j)
            with pool.Fori(1, TOK // P) as g:
                pool.wait_ge(z_done, g)
                for j in range(GB):
                    gather(g * GB + j, j)

        def act_layer1(act, f, n0):
            if f % 2 == 0 and f // 2 < G:
                n = n0 + f // 2
                act.wait_ge(x1t_ps, n + 1)
                act.wait_ge(z_done, n)
                act.activation(x1t[:, :, :], s_ps[:, :].rearrange("p (c t) -> p c t", c=C), ACT.Copy).then_inc(x1t_done, 1)
            if f % 2 == 0 and 0 <= f // 2 - 1 < G:
                n = n0 + (f // 2 - 1)
                act.wait_ge(wht_ps, n + 1)
                act.wait_ge(o_done, n)
                act.activation(wht[:, :], z_ps[:, 256:256 + P], ACT.Copy).then_inc(wht_done, 1)

        def act_split_w(act, f):
            act.wait_ge(stage_in[f % 4], 16 * (f // 4 + 1))
            act.activation(w_hi[:, f, :, :, :].rearrange("p g c k -> p (g c k)"), stage[:, f % 4, :], ACT.Copy).then_inc(whi_done, 1)

        def act_split_y(act, t):
            for i in range(C):
                act.activation(y_hi[:, i, :].rearrange("p (b h) -> p b h", h=H),
                               uy[:, :, i, bass.ds(t * BT, BT)].rearrange("p h b -> p b h"), ACT.Copy).then_inc(yhi_done, 1)

        def act_tile(act, t, first_tile):
            for f in range(F):
                n = t * F + f
                act.wait_ge(gate_done, n + 1)
                if not (first_tile and f == 0):
                    act.wait_ge(prod_done, n)
                act.activation(gate_sb[:, :], gate_ps[:, :], ACT.Silu).then_inc(silu_done, 1)
                if first_tile and f + 2 < F:
                    act_split_w(act, f + 2)
                if not (first_tile and f < 2):
                    act.wait_ge(down_done, n - 1 if f else n)
                act.activation(wd_hi[:, f % 2, :], wd_raw[:, f, :], ACT.Copy).then_inc(wdhi_done, 1)
                act.wait_ge(prod_done, n + 1)
                act.activation(h_hi[:, f % 2, :], prod_sb[:, :], ACT.Copy).then_inc(hhi_done, 1)
                if not first_tile:
                    act_layer1(act, f, t * G - G)

        @block.scalar
        def _(act):
            act.wait_ge(s4, 1)
            act.activation(small[:, 18:20, :], small[:, 16:18, :], ACT.Sin, scale=TWO_PI).then_inc(sin_done, 1)
            act.activation(small[:, 20, :], small[:, 16, :], ACT.Sin, scale=TWO_PI / 2).then_inc(sin_done, 1)
            act.wait_ge(s4, 2)
            act.activation(phase[:, :], phase[:, :], ACT.Sin, scale=TWO_PI).then_inc(sin_done, 1)
            act.activation(expo[:, :], expo[:, :], ACT.Exp).then_inc(exp_done, 1)
            with act.Fori(0, E // 2) as i:
                for s in range(2):
                    act.wait_ge(aw_done, i * 2 + s + 1)
                    act.wait_ge(aw_out[s], i * 16)
                    for k in range(2):
                        last = act.activation(aw_sb[:, s, 2 * k:2 * k + 2, :].rearrange("p c z -> p (c z)"),
                                              aw_ps[s][k][:, 0:2 * Z], ACT.Copy)
                        last.then_inc(aw_copied, 1)
                    act.wait_ge(aw_copied, i * 4 + 2 * s + 2)
                    act.dma_start(aw_dram[:, bass.ds(i * (2 * C * Z) + s * (C * Z), C * Z)],
                                  aw_sb[:, s, :, :].rearrange("p c z -> p (c z)")).then_inc(aw_out[s], 16)
            for f in range(2):
                act_split_w(act, f)
            act.wait_ge(y_done, PAIRS)
            act.wait_ge(conv_done, PAIRS)
            act_split_y(act, 0)
            act.wait_ge(wd_in, 16)
            act_tile(act, 0, True)
            with act.Fori(1, NT) as t:
                act.wait_ge(up_done, t * F)
                act_split_y(act, t)
                act_tile(act, t, False)
            for f in range(SLOTS):
                act_layer1(act, f, (NT - 1) * G)

        def dve_layer1(dve, f, n0):
            if f % 2 == 1 and f // 2 < G:
                n = n0 + f // 2
                dve.wait_ge(z_done, n + 1)
                dve.wait_ge(wh_done, n)
                dve.tensor_reduce(mx[:, :], z_ps[:, 0:E], AX_X, ALU.max).then_inc(route, 1)
                dve.wait_ge(route, n * 4 + 1)
                dve.scalar_tensor_tensor(out=cand[:, :], in0=z_ps[:, 0:E], scalar=mx[:, 0:1],
                                         in1=con[:, K_RANK:K_RANK + E], op0=ALU.is_ge, op1=ALU.mult).then_inc(route, 1)
                dve.wait_ge(route, n * 4 + 2)
                dve.tensor_reduce(first[:, :], cand[:, :], AX_X, ALU.max).then_inc(route, 1)
                dve.wait_ge(route, n * 4 + 3)
                dve.tensor_scalar(rw[:, :], cand[:, :], first[:, 0:1], mx[:, 0:1], ALU.is_equal, ALU.mult).then_inc(route, 1)
                dve.wait_ge(route, n * 4 + 4)
                dve.wait_ge(wht_ps, n)
                dve.tensor_tensor(wh[:, :].rearrange("p (e r) -> p e r", e=E),
                                  z_ps[:, E:Z].rearrange("p (e r) -> p e r", e=E),
                                  rw[:, :].unsqueeze(2).to_broadcast([P, E, R]), ALU.mult).then_inc(wh_done, 1)
            if f % 2 == 1 and 0 <= f // 2 - 1 < G:
                g = f // 2 - 1
                n = n0 + g
                dve.wait_ge(o_done, n + 1)
                dve.tensor_tensor(x1[:, g, :], s_ps[:, :], x1[:, g, :], ALU.add).then_inc(out_ready, 1)

        def dve_split_w(dve, f):
            dve.wait_ge(whi_done, f + 1)
            dve.tensor_tensor(w_lo[:, f, :, :, :].rearrange("p g c k -> p (g c k)"), stage[:, f % 4, :],
                              w_hi[:, f, :, :, :].rearrange("p g c k -> p (g c k)").bitcast(F32), ALU.subtract).then_inc(wlo_done, 1)

        def dve_split_y(dve, t):
            for i in range(C):
                dve.wait_ge(yhi_done, t * C + i + 1)
                dve.tensor_tensor(y_lo[:, i, :].rearrange("p (b h) -> p b h", h=H),
                                  uy[:, :, i, bass.ds(t * BT, BT)].rearrange("p h b -> p b h"),
                                  y_hi[:, i, :].rearrange("p (b h) -> p b h", h=H).bitcast(F32), ALU.subtract).then_inc(ylo_done, 1)

        def dve_tile(dve, t, first_tile):
            for f in range(F):
                n = t * F + f
                dve.wait_ge(silu_done, n + 1)
                dve.wait_ge(up_done, n + 1)
                if not (first_tile and f == 0):
                    dve.wait_ge(hhi_done, n)
                    dve.wait_ge(hlo_done, n)
                dve.tensor_tensor(prod_sb[:, :], gate_sb[:, :], up_ps[:, :], ALU.mult).then_inc(prod_done, 1)
                dve.wait_ge(wdhi_done, n + 1)
                dve.tensor_tensor(wd_lo[:, f % 2, :], wd_raw[:, f, :], wd_hi[:, f % 2, :].bitcast(F32), ALU.subtract).then_inc(wdlo_done, 1)
                dve.wait_ge(hhi_done, n + 1)
                dve.tensor_tensor(h_lo[:, f % 2, :], prod_sb[:, :], h_hi[:, f % 2, :].bitcast(F32), ALU.subtract).then_inc(hlo_done, 1)
                if first_tile and f + 2 < F:
                    dve_split_w(dve, f + 2)
                if not first_tile:
                    dve_layer1(dve, f, t * G - G)

        def dve_x1(dve, t):
            for g in range(G):
                dve.wait_ge(down_done, t * F + F)
                dve.wait_ge(xn_in[g % 2], t * (8 * G) + 16 * (g // 2 + 1))
                dve.wait_ge(out_done[g], t * 16)
                dve.tensor_tensor(x1[:, g, :], down_ps[g][:, :], xn_sb[:, g % 2, :], ALU.add).then_inc(x1_done, 1)

        def dve_s4d(dve):
            chain = [0]
            s4d_step = sem("s4d_step")

            def link(ins):
                chain[0] += 1
                ins.then_inc(s4d_step, 1)
                dve.wait_ge(s4d_step, chain[0])

            def S(i, w=1):
                return small[:, i:i + w, :]

            def tt(o, a, b, op):
                link(dve.tensor_tensor(o, a, b, op))

            def ts(o, a, s1, s2, op0, op1=ALU.bypass):
                link(dve.tensor_scalar(o, a, s1, s2, op0, op1) if s2 is not None else dve.tensor_scalar(o, a, s1, None, op0))

            def stt(o, a, s, b, op0, op1):
                flat = "p a h -> p (a h)"
                link(dve.scalar_tensor_tensor(out=o.rearrange(flat), in0=a.rearrange(flat), scalar=s, in1=b.rearrange(flat), op0=op0, op1=op1))

            def exp_parts(x, w, t, k, p, s):
                ts(x, x, -87.0, 88.7, ALU.max, ALU.min)
                ts(k, x, LOG2E, ROUND, ALU.mult, ALU.add)
                ts(k, k, ROUND, None, ALU.subtract)
                stt(t, k, -LN2_HI, x, ALU.mult, ALU.add)
                stt(t, k, -LN2_LO, t, ALU.mult, ALU.add)
                fact = [1.0, 2.0, 6.0, 24.0, 120.0, 720.0, 5040.0, 40320.0]
                ts(p, t, 1.0 / fact[7], None, ALU.mult)
                for m in range(6, -1, -1):
                    stt(p, p, 1.0 / fact[m], t, ALU.add, ALU.mult)
                ts(s.bitcast(I32), k, 127.0, None, ALU.add)
                ts(s.bitcast(I32), s.bitcast(I32), 23, None, ALU.logical_shift_left)

            dve.wait_ge(par_in, 16)
            x2 = par[:, 0:2, :]
            exp_parts(x2, 2, S(0, 2), S(2, 2), S(4, 2), S(6, 2))
            stt(S(4, 2), S(4, 2), 1.0, S(6, 2), ALU.add, ALU.mult)
            dt, ar, ai = S(4), S(5), par[:, 2:3, :]
            al, w_ = S(8), S(9)
            stt(al, ar, -1.0, dt, ALU.mult, ALU.mult)
            tt(w_, ai, dt, ALU.mult)
            ts(S(10), w_, INV_2PI, None, ALU.mult)
            ts(S(11), S(10), ROUND, ROUND, ALU.add, ALU.subtract)
            tt(S(16), S(10), S(11), ALU.subtract)
            ts(S(12), S(16), 0.25, ROUND, ALU.add, ALU.add)
            ts(S(12), S(12), ROUND, -0.25, ALU.subtract, ALU.add)
            dve.tensor_tensor(S(17), S(16), S(12), ALU.subtract).then_inc(s4, 1)
            f0 = S(16)
            ts(S(13), f0, float(NB), None, ALU.mult)
            ts(S(14), S(13), ROUND, ROUND, ALU.add, ALU.subtract)
            tt(S(15), S(13), S(14), ALU.subtract)

            def over(i, n):
                return small[:, i, :].unsqueeze(2).to_broadcast([P, H, n])

            def index(k, n):
                return con[:, k:k + n].unsqueeze(1).to_broadcast([P, H, n])

            def tab(t, at_, n):
                return t[:, at_:at_ + H * n].rearrange("p (h n) -> p h n", n=n)

            dve.wait_ge(con_in, 64)
            tt(tab(phase, 0, NA), over(15, NA), index(K_A, NA), ALU.mult)
            ts(phase[:, 512:1024], phase[:, 0:512], 0.25, None, ALU.add)
            tt(tab(phase, 1024, NB), over(16, NB), index(K_B, NB), ALU.mult)
            ts(phase[:, 1024:2048], phase[:, 1024:2048], con[:, K_OFF:K_OFF + 1], None, ALU.add)
            ts(whole[:, :], phase[:, :], ROUND, ROUND, ALU.add, ALU.subtract)
            tt(phase[:, :], phase[:, :], whole[:, :], ALU.subtract)
            ts(S(13), al, float(NB), None, ALU.mult)
            tt(tab(expo, 0, NA), over(13, NA), index(K_A, NA), ALU.mult)
            dve.tensor_tensor(tab(expo, 512, NB), over(8, NB), index(K_B, NB), ALU.mult).then_inc(s4, 1)
            ts(S(21), al, 1.0, None, ALU.mult)
            exp_parts(S(21), 1, S(22), S(23), S(24), S(25))
            tt(S(24), S(24), S(25), ALU.mult)
            ts(S(25), S(25), -1.0, None, ALU.add)
            tt(S(24), S(24), S(25), ALU.add)
            em = S(24)
            dve.wait_ge(sin_done, 2)
            siny, cosy, sinh = S(18), S(19), S(20)
            tt(S(26), em, cosy, ALU.mult)
            tt(S(27), sinh, sinh, ALU.mult)
            stt(S(26), S(27), -2.0, S(26), ALU.mult, ALU.add)
            stt(S(27), em, 1.0, siny, ALU.add, ALU.mult)
            nr, ni = S(26), S(27)
            tt(S(28), ar, ar, ALU.mult)
            tt(S(29), ai, ai, ALU.mult)
            tt(S(28), S(28), S(29), ALU.add)
            link(dve.reciprocal(S(28), S(28)))
            tt(S(29), nr, ar, ALU.mult)
            tt(S(30), ni, ai, ALU.mult)
            tt(S(29), S(30), S(29), ALU.subtract)
            tt(S(29), S(29), S(28), ALU.mult)
            tt(S(30), nr, ai, ALU.mult)
            tt(S(31), ni, ar, ALU.mult)
            tt(S(30), S(30), S(31), ALU.add)
            stt(S(30), S(30), -1.0, S(28), ALU.mult, ALU.mult)
            gr, gi = S(29), S(30)
            c1, c2 = par[:, 3:4, :], par[:, 4:5, :]
            ts(c2, c2, con[:, K_SIGN:K_SIGN + 1], None, ALU.mult)
            tt(S(31), c1, gr, ALU.mult)
            tt(S(32), c2, gi, ALU.mult)
            tt(S(31), S(31), S(32), ALU.subtract)
            ts(S(31), S(31), 2.0, None, ALU.mult)
            tt(S(32), c1, gi, ALU.mult)
            tt(S(33), c2, gr, ALU.mult)
            tt(S(32), S(32), S(33), ALU.add)
            ts(S(32), S(32), -2.0, None, ALU.mult)
            dve.wait_ge(sin_done, 3)
            tt(u_tab[:, :, :], tab(phase, 512, NA), over(31, NA), ALU.mult)
            tt(q_tab[:, :, :], tab(phase, 0, NA), over(32, NA), ALU.mult)
            tt(u_tab[:, :, :], u_tab[:, :, :], q_tab[:, :, :], ALU.add)
            dve.wait_ge(exp_done, 1)
            tt(u_tab[:, :, :], u_tab[:, :, :], tab(expo, 0, NA), ALU.mult)
            dve.tensor_tensor(v_tab[:, :, :], tab(phase, 1024, NB), tab(expo, 512, NB), ALU.mult).then_inc(tab_done, 1)

        @block.vector
        def _(dve):
            dve_s4d(dve)
            for i in range(C):
                last = dve.tensor_scalar(mask[:, i, :], len_sb[:, :], con[:, K_L + i:K_L + i + 1], None, ALU.is_gt)
            last.then_inc(mask_done, 1)
            dve.tensor_scalar(id_neg[:, :], id_sb[:, :], 0.0, float(E), ALU.is_lt, ALU.mult).then_inc(mask_done, 1)
            dve.wait_ge(mask_done, 2)
            dve.tensor_tensor(id_fit[:, :], id_sb[:, :], id_neg[:, :], ALU.add).then_inc(mask_done, 1)
            dve.wait_ge(mask_done, 3)
            dve.tensor_scalar(id_row[:, :], id_fit[:, :], 0.0, float(E - 1), ALU.max, ALU.min).then_inc(ids_done, 1)
            dve.memset(zero[:, :], 0.0).then_inc(k_ready, 1)
            dve.wait_ge(k_done, 1)
            for i in range(2):
                last = dve.tensor_copy(k_sb[:, i * (H // 2):(i + 1) * (H // 2), :].rearrange("a h b -> a (h b)"), k_ps[i][0:NA, :])
            last.then_inc(mask_done, 1)
            dve.wait_ge(mask_done, 4)
            dve.tensor_tensor(k_sb[0:1, :, 0], k_sb[0:1, :, 0], dk_sb[:, :], ALU.add).then_inc(k_ready, 1)
            for f in range(2):
                dve_split_w(dve, f)
            with dve.Fori(0, PAIRS // 4) as i:
                for s in range(4):
                    dve.wait_ge(conv_done, i * 4 + s + 1)
                    dve.tensor_tensor(uy[:, bass.ds(i * 8 + 2 * s, 2), :, :].rearrange("p h c b -> p h (c b)"),
                                      down_ps[s][:, :].rearrange("p (h k) -> p h k", h=2),
                                      mask[:, :, :].rearrange("p c b -> p (c b)").unsqueeze(1).to_broadcast([P, 2, C * B]),
                                      ALU.mult).then_inc(y_done, 1)
            dve.wait_ge(y_done, PAIRS)
            dve_split_y(dve, 0)
            dve_tile(dve, 0, True)
            with dve.Fori(1, NT) as t:
                dve.wait_ge(up_done, t * F)
                dve_split_y(dve, t)
                dve_x1(dve, t - 1)
                dve_tile(dve, t, False)
            dve_x1(dve, NT - 1)
            for f in range(SLOTS):
                dve_layer1(dve, f, (NT - 1) * G)

        def pe_layer1(pe, f, n0):
            if f % 2 == 0 and f // 2 < G:
                g = f // 2
                n = n0 + g
                pe.wait_ge(x1_done, n + 1)
                pe.wait_ge(out_ready, n - 1 if g else n)
                for c in range(C):
                    last = pe.transpose(s_ps[:, c * P:(c + 1) * P], x1[:, g, c * P:(c + 1) * P], ident)
                last.then_inc(x1t_ps, 1)
            if f % 2 == 0 and 0 <= f // 2 - 1 < G:
                n = n0 + (f // 2 - 1)
                pe.wait_ge(wh_done, n + 1)
                pe.transpose(z_ps[:, 256:256 + P], wh[:, :], ident).then_inc(wht_ps, 1)
            if f % 2 == 1 and f // 2 < G:
                n = n0 + f // 2
                pe.wait_ge(x1t_done, n + 1)
                pe.wait_ge(wht_done, n)
                for j in range(GB):
                    pe.wait_ge(mb_in[j], n * 16 + 16)
                for c in range(C):
                    for j in range(GB):
                        last = pe.matmul(z_ps[H * j:H * j + H, 0:Z], x1t[:, c, H * j:H * j + H], mb[:, j, c, :],
                                         start=(c == 0), stop=(c == C - 1), tile_position=(0, H * j))
                last.then_inc(z_done, 1)
            if f % 2 == 1 and 0 <= f // 2 - 1 < G:
                n = n0 + (f // 2 - 1)
                pe.wait_ge(wht_done, n + 1)
                pe.wait_ge(x1t_done, n + 2 if f // 2 < G else n + 1)
                pe.wait_ge(out_ready, n)
                pe.matmul(s_ps[:, :], wht[:, :], b2_sb[:, :], start=True, stop=True).then_inc(o_done, 1)

        def pe_gate_up(pe, bank, f, k):
            for c in range(C):
                pe.matmul(bank[:, :], w_hi[:, f, k, c, :], y_hi[:, c, :], start=(c == 0), stop=False)
                pe.matmul(bank[:, :], w_hi[:, f, k, c, :], y_lo[:, c, :], start=False, stop=False)
                last = pe.matmul(bank[:, :], w_lo[:, f, k, c, :], y_hi[:, c, :], start=False, stop=(c == C - 1))
            return last

        def pe_down(pe, n, f):
            pe.wait_ge(wdhi_done, n + 1)
            pe.wait_ge(wdlo_done, n + 1)
            pe.wait_ge(hhi_done, n + 1)
            pe.wait_ge(hlo_done, n + 1)
            for g in range(G):
                tok = slice(g * P, (g + 1) * P)
                pe.matmul(down_ps[g][:, :], h_hi[:, f % 2, tok], wd_hi[:, f % 2, :], start=(f == 0), stop=False)
                pe.matmul(down_ps[g][:, :], h_hi[:, f % 2, tok], wd_lo[:, f % 2, :], start=False, stop=False)
                last = pe.matmul(down_ps[g][:, :], h_lo[:, f % 2, tok], wd_hi[:, f % 2, :], start=False, stop=(f == F - 1))
            last.then_inc(down_done, 1)

        def pe_tile(pe, t, first_tile):
            pe.wait_ge(yhi_done, t * C + C)
            pe.wait_ge(ylo_done, t * C + C)
            for f in range(F):
                n = t * F + f
                if first_tile:
                    pe.wait_ge(whi_done, f + 1)
                    pe.wait_ge(wlo_done, f + 1)
                if not (first_tile and f == 0):
                    pe.wait_ge(silu_done, n)
                pe_gate_up(pe, gate_ps, f, 0).then_inc(gate_done, 1)
                if not (first_tile and f == 0):
                    pe.wait_ge(prod_done, n)
                pe_gate_up(pe, up_ps, f, 1).then_inc(up_done, 1)
                if f == 1 and not first_tile:
                    pe.wait_ge(x1_done, t * G)
                if f:
                    pe_down(pe, n - 1, f - 1)
                if not first_tile:
                    pe_layer1(pe, f, t * G - G)
            pe_down(pe, t * F + (F - 1), F - 1)

        @block.tensor
        def _(pe):
            pe.wait_ge(ra_in, 16)
            with pe.Fori(0, E // 4) as i:
                for s in range(4):
                    pe.wait_ge(we_in[s], i * 16 + 16)
                    pe.wait_ge(aw_copied, i * 8 + max(0, 2 * s - 2))
                    for ic in range(C):
                        bank = aw_ps[s % 2][ic // 2]
                        for oc in range(C):
                            last = pe.matmul(bank[:, (ic % 2) * Z:(ic % 2 + 1) * Z], we_sb[:, s, oc, ic * P:(ic + 1) * P],
                                             ra_sb[:, oc, :], start=(oc == 0), stop=(oc == C - 1))
                    last.then_inc(aw_done, 1)
            pe.wait_ge(tab_done, 1)
            for h in range(H):
                bank = k_ps[h // (H // 2)]
                col = (h % (H // 2)) * NB
                last = pe.matmul(bank[0:NA, col:col + NB], u_tab[:, h, :], v_tab[:, h, :], start=True, stop=True)
            last.then_inc(k_done, 1)
            for q in range(4):
                pe.wait_ge(ut_in[q], 16)
            pe.wait_ge(k_ready, 2)

            def conv(pair, s, peeled):
                pe.wait_ge(toep_in[s], (pair - s) * 4 + 16)
                if not peeled:
                    pe.wait_ge(y_done, pair - 3)
                for k in range(2):
                    for d in range(C):
                        last = pe.matmul(down_ps[s][:, k * C * B + d * B:(k + 1) * C * B], toep[:, s, k, d * P:(d + 1) * P],
                                         uy[:, bass.ds(pair * 2 + k, 1), 0:C - d, :].rearrange("p h c b -> p (h c b)"),
                                         start=(k == 0 and d == 0), stop=(d == C - 1), skip_group_check=True)
                last.then_inc(conv_done, 1)

            for s in range(4):
                conv(s, s, True)
            with pe.Fori(1, PAIRS // 4) as i:
                for s in range(4):
                    conv(i * 4 + s, s, False)
            pe_tile(pe, 0, True)
            with pe.Fori(1, NT) as t:
                pe_tile(pe, t, False)
            for f in range(SLOTS):
                pe_layer1(pe, f, (NT - 1) * G)


def kernel(**inputs):
    import numpy as np
    import concourse.bacc as bacc
    from concourse.bass_utils import run_bass_kernel_spmd

    def a(name):
        return np.asarray(inputs[name])

    x = a("x")
    ut = x.reshape(B, H, C, P)[:, :, :, ::-1].transpose(3, 1, 2, 0)

    def pad(w):
        return np.pad(w, ((0, F * P - D_FF), (0, 0)))

    wgu = np.stack([pad(a(n)).reshape(F, P, C, P).transpose(0, 3, 2, 1) for n in ("L0_ffn_W_gate", "L0_ffn_W_up")], 2)
    wd = pad(a("L0_ffn_W_down").T).reshape(F, P, L).transpose(1, 0, 2)
    we = a("L1_cond_weight").reshape(E, C, P, L).transpose(0, 2, 1, 3)
    ra = np.concatenate([a("L1_ffn_route_w"), a("L1_ffn_A").reshape(ER, L)]).T.reshape(C, P, Z).transpose(1, 0, 2)
    b2 = a("L1_ffn_Bw").transpose(0, 2, 1).reshape(ER, L)
    re, im = a("L0_cond_C")[..., 0].T, a("L0_cond_C")[..., 1].T

    def twice(m):
        return np.concatenate([m, m])

    params = np.stack([np.broadcast_to(a("L0_cond_log_dt"), (P, H)), twice(a("L0_cond_log_A_real").T), twice(a("L0_cond_A_imag").T),
                       np.concatenate([re, im]), np.concatenate([im, re])], 1)
    consts = np.zeros((P, K_END), np.float32)
    consts[:, K_ID:K_ID + P] = np.eye(P)
    consts[:, K_A:K_A + NA] = np.arange(NA)
    consts[:, K_B:K_B + NB] = np.arange(NB)
    consts[:, K_L:K_L + C] = np.arange(L).reshape(C, P).T
    consts[:, K_SIGN] = np.repeat([1, -1], N_STATE)
    consts[:, K_OFF] = np.repeat([0.25, 0.5], N_STATE)
    consts[:, K_RANK:K_RANK + E] = E - np.arange(E)
    arrays = {
        "params": params, "consts": consts, "d_skip": a("L0_cond_D").reshape(1, H),
        "lens": np.broadcast_to(a("itok_B_8_3872"), (P, B)), "ids": a("itok_B_3_7").reshape(1, B),
        "ut": ut, "xn": x.reshape(TOK // P, P, L), "wgu": wgu.reshape(F, P, 2 * C * P), "wd": wd, "we": we, "ra": ra, "b2": b2,
    }
    nc = bacc.Bacc("TRN2", target_bir_lowering=False, num_devices=1)
    arrays = {k: np.ascontiguousarray(v) for k, v in arrays.items()}
    aps = {k: nc.dram_tensor(k, v.shape, mybir.dt.from_np(v.dtype), kind="ExternalInput").ap() for k, v in arrays.items()}
    out = nc.dram_tensor("out", (TOK // P, P, L), F32, kind="ExternalOutput").ap()
    build(nc, out=out, **aps)
    r = run_bass_kernel_spmd(nc, [arrays], core_ids=[0])
    return r.results[0]["out"].reshape(B, H, L)
```

```python
from contextlib import ExitStack

import concourse.bass as bass
from concourse import mybir

ALU = mybir.AluOpType
ACT = mybir.ActivationFunctionType
F32 = mybir.dt.float32
F32R = mybir.dt.float32r
I32 = mybir.dt.int32
AX_X = mybir.AxisListType.X

P = 128
B, H, L = 64, 32, 512
N_STATE = 64
D_FF = 1376
E, R = 8, 16
C = L // P
F = -(-D_FF // P)
ER = E * R
Z = E + ER
NA = 16
NB = L // NA
TOK = B * H
TILE = 512
NT = TOK // TILE
BT = TILE // H
G = TILE // P
GB = P // H
PAIRS = H // 2
KROW = P + L

K_ID, K_A, K_B, K_L, K_SIGN, K_OFF, K_RANK, K_END = 0, 128, 144, 176, 180, 181, 182, 190

LOG2E = 1.4426950408889634
LN2_HI = 0.693359375
LN2_LO = -2.12194440054690583e-4
FREE = 1
ROUND = 12582912.0
INV_2PI = 0.15915494309189535
TWO_PI = 6.283185


def build(nc, params, consts, d_skip, lens, ids, ut, xn, wgu, wd, we, ra, b2, out):
    ctx = ExitStack()
    with ctx:
        at = [16512]

        def sb(name, shape, dt, off=None):
            size = 4
            for n in shape[1:]:
                size *= n
            if off is None:
                off, at[0] = at[0], at[0] + -(-size // 32) * 32
            return nc.alloc_sbuf_tensor_at(name, shape, dt, offset=off)

        def region(size):
            off, at[0] = at[0], at[0] + size
            return off

        def sem(name):
            return ctx.enter_context(nc.semaphore(name))

        def ps(name):
            return ctx.enter_context(nc.psum_tensor(name, [P, 512], F32))

        r_whi, r_wlo = region(F * 4096), region(F * 4096)
        r_wd, r_uy, r_y = region(F * 2048), region(H * 1024), region(16384)
        r_h, r_wds, r_gt = region(8192), region(8192), region(4096)
        r_x1, r_mb = region(8192), region(GB * C * Z * 4)
        r_xn = region(4096 + 2048 + 3 * 512)
        w_hi = sb("w_hi", [P, F, 2, C, P], F32R, r_whi)
        w_lo = sb("w_lo", [P, F, 2, C, P], F32R, r_wlo)
        wd_raw = sb("wd_raw", [P, F, L], F32, r_wd)
        uy = sb("uy", [P, H, C, B], F32, r_uy)
        y_hi = sb("y_hi", [P, C, TILE], F32R, r_y)
        y_lo = sb("y_lo", [P, C, TILE], F32R, r_y + 8192)
        h_hi = sb("h_hi", [P, 2, TILE], F32R, r_h)
        h_lo = sb("h_lo", [P, 2, TILE], F32R, r_h + 4096)
        wd_hi = sb("wd_hi", [P, 2, L], F32R, r_wds)
        wd_lo = sb("wd_lo", [P, 2, L], F32R, r_wds + 4096)
        gate_sb = sb("gate_sb", [P, TILE], F32, r_gt)
        prod_sb = sb("prod_sb", [P, TILE], F32, r_gt + 2048)
        x1 = sb("x1", [P, G, L], F32, r_x1)
        mb = sb("mb", [P, GB, C, Z], F32, r_mb)
        xn_sb = sb("xn_sb", [P, 2, L], F32, r_xn)
        x1t = sb("x1t", [P, C, P], F32, r_xn + 4096)
        wh = sb("wh", [P, ER], F32, r_xn + 6144)
        wht_hi = sb("wht_hi", [P, P], F32R, r_xn + 6656)
        wht_lo = sb("wht_lo", [P, P], F32R, r_xn + 7168)
        b2_hi = sb("b2_hi", [P, L], F32R)
        b2_lo = sb("b2_lo", [P, L], F32R)
        con = sb("con", [P, K_END], F32)
        id_sb = sb("id_sb", [1, B], I32)
        id_row = sb("id_row", [1, B], I32)
        mx = sb("mx", [P, G, 1], F32)
        cand = sb("cand", [P, G, E], F32)
        first = sb("first", [P, G, 1], F32)
        rw = sb("rw", [P, G, E], F32)
        dk_sb = sb("dk_sb", [1, H], F32)
        toep = sb("toep", [P, 4, 2, L], F32, r_y)
        we_sb = sb("we_sb", [P, 4, C, L], F32, r_wlo + 3 * 4096)
        stage = sb("stage", [P, 4, 2 * C * P], F32, r_x1)
        aw_sb = sb("aw_sb", [P, 2, C, Z], F32, r_xn)
        ra_sb = sb("ra_sb", [P, C, Z], F32, r_xn + 4352)
        phase = sb("phase", [P, 2048], F32, r_wd)
        whole = sb("whole", [P, 2048], F32, r_wd + 8192)
        expo = sb("expo", [P, 1536], F32, r_wd + 16384)
        u_tab = sb("u_tab", [P, H, NA], F32, r_h)
        v_tab = sb("v_tab", [P, H, NB], F32, r_h + 2048)
        q_tab = sb("q_tab", [P, H, NA], F32, r_h + 6144)
        k_sb = sb("k_sb", [NA, H, NB], F32, r_gt)
        par = sb("par", [P, 5, H], F32, r_wds)
        small = sb("small", [P, 40, H], F32, r_wds + 640)
        b2_raw = sb("b2_raw", [P, L], F32, r_wds + 5760)
        len_sb = sb("len_sb", [P, B], I32, r_wds + 7808)
        mask = sb("mask", [P, C, B], F32, r_h + 6144)
        id_neg = small[0:1, 36:38, :].rearrange("p a h -> p (a h)")
        id_fit = small[0:1, 38:40, :].rearrange("p a h -> p (a h)")
        mb_end = sb("mb_end", [P, G - 1, GB, C, Z], F32, r_uy)
        x1t_end = sb("x1t_end", [P, G, C, P], F32, r_y)
        wh_end = sb("wh_end", [P, G, ER], F32, r_y + 8192)
        wht_hi_end = sb("wht_hi_end", [P, G, P], F32R, r_y + 10240)
        wht_lo_end = sb("wht_lo_end", [P, G, P], F32R, r_y + 12288)
        assert at[0] <= nc.sbuf_top
        zero = sb("zero", [H, P], F32, r_mb + GB * C * Z * 4 - 512)
        ident = con[:, K_ID:K_ID + P]

        gate_ps, up_ps = ps("gate_ps"), ps("up_ps")
        down_ps = [ps(f"down_ps{g}") for g in range(G)]
        s_ps, z_ps = ps("s_ps"), ps("z_ps")
        end_ps = [gate_ps, up_ps, s_ps, z_ps]
        aw_ps = [[gate_ps, up_ps], [s_ps, z_ps]]
        k_ps = down_ps[0:2]

        k_dram = nc.dram_tensor("k_dram", [H, KROW], F32)
        aw_dram = nc.dram_tensor("aw_dram", [P, E * C * Z], F32)

        par_in, con_in, ra_in, b2_in, wd_in = sem("par_in"), sem("con_in"), sem("ra_in"), sem("b2_in"), sem("wd_in")
        we_half = [sem(f"we_half{i}") for i in range(2)]
        we_in = [sem(f"we_in{i}") for i in range(4)]
        ut_in = [sem(f"ut_in{i}") for i in range(4)]
        toep_in = [sem(f"toep_in{i}") for i in range(4)]
        stage_in = [sem(f"stage_in{i}") for i in range(4)]
        xn_in = [sem(f"xn_in{i}") for i in range(2)]
        mb_in = [sem(f"mb_in{i}") for i in range(GB)]
        out_done = [sem(f"out_done{g}") for g in range(G)]
        k_out, aw_out = sem("k_out"), [sem(f"aw_out{i}") for i in range(2)]
        s4d, s4d_em, sin_done, expo_done, exp_done = sem("s4d"), sem("s4d_em"), sem("sin_done"), sem("expo_done"), sem("exp_done")
        s4d_at = {}
        u_done, v_done = sem("u_done"), sem("v_done")
        k_done, k_ready, mask_done, ids_done = sem("k_done"), sem("k_ready"), sem("mask_done"), sem("ids_done")
        aw_done, aw_copied = sem("aw_done"), sem("aw_copied")
        conv_done, y_done = sem("conv_done"), sem("y_done")
        whi_done, wlo_done = sem("whi_done"), sem("wlo_done")
        yhi_done, ylo_done = sem("yhi_done"), sem("ylo_done")
        gate_done, up_done, down_done = sem("gate_done"), sem("up_done"), sem("down_done")
        silu_done, prod_done = sem("silu_done"), sem("prod_done")
        hhi_done, hlo_done, wdhi_done, wdlo_done = sem("hhi_done"), sem("hlo_done"), sem("wdhi_done"), sem("wdlo_done")
        x1_done, x1t_ps, x1t_done = sem("x1_done"), sem("x1t_ps"), sem("x1t_done")
        z_done, wh_done, wht_ps, wht_done = sem("z_done"), sem("wh_done"), sem("wht_ps"), sem("wht_done")
        whtlo_done, b2hi_done, b2lo_done, end_down = sem("whtlo_done"), sem("b2hi_done"), sem("b2lo_done"), sem("end_down")
        o_done, out_ready, route = sem("o_done"), sem("out_ready"), sem("route")

        def over(i, n):
            return small[:, i, :].unsqueeze(2).to_broadcast([P, H, n])

        def index(k, n):
            return con[:, k:k + n].unsqueeze(1).to_broadcast([P, H, n])

        def tab(t, at_, n):
            return t[:, at_:at_ + H * n].rearrange("p (h n) -> p h n", n=n)

        END_ORDER = [(0, "down"), (0, "x1"), (1, "down"), (1, "x1"), (0, "x1t"), (2, "down"), (2, "x1"), (1, "x1t"), (0, "z"),
                     (3, "down"), (3, "x1"), (2, "x1t"), (1, "z"), (0, "wht"), (3, "x1t"), (2, "z"), (0, "out"), (1, "wht"),
                     (3, "z"), (1, "out"), (2, "wht"), (2, "out"), (3, "wht"), (3, "out")]

        block = ctx.enter_context(nc.Block())

        @block.sync
        def _(sp):
            sp.dma_start(par[:, :, :], params).then_inc(par_in, 16)
            sp.dma_start(ra_sb[:, :, :], ra).then_inc(ra_in, 16)
            for k in range(2):
                sp.dma_start(we_sb[:, 0, :, k * (L // 2):(k + 1) * (L // 2)],
                             we[0][:, :, k * (L // 2):(k + 1) * (L // 2)]).then_inc(we_half[k], 16)
            sp.dma_start(con[:, :], consts).then_inc(con_in, 16)
            sp.dma_start(dk_sb[:, :], d_skip).then_inc(con_in, 16)
            sp.dma_start(len_sb[:, :], lens).then_inc(con_in, 16)
            sp.dma_start(id_sb[:, :], ids).then_inc(con_in, 16)
            for e in range(1, 4):
                sp.dma_start(we_sb[:, e, :, :], we[e]).then_inc(we_in[e], 16)

            def load_u(q):
                sp.dma_start(uy[:, 8 * q:8 * q + 8, :, :], ut[:, 8 * q:8 * q + 8]).then_inc(ut_in[q], 16)

            def load_we(e):
                sp.wait_ge(aw_done, e - 3)
                sp.dma_start(we_sb[:, e % 4, :, :], we[e]).then_inc(we_in[e % 4], 16)

            load_u(0)
            load_u(1)
            load_we(4)
            load_we(5)
            sp.wait_ge(k_ready, 2)
            sp.dma_start(k_dram[:, 0:P], zero[:, :]).then_inc(k_out, 16)
            sp.dma_start(k_dram[:, P:KROW].rearrange("h (a b) -> a h b", a=NA), k_sb[:, :, :]).then_inc(k_out, 16)
            load_we(6)
            sp.wait_ge(k_out, 32)

            def load_toep(pair):
                if pair >= 4:
                    sp.wait_ge(conv_done, pair - 3)
                sp.dma_start(toep[:, pair % 4, :, :],
                             bass.AP(k_dram, pair * 2 * KROW + 1, [[1, P], [KROW, 2], [1, L]])).then_inc(toep_in[pair % 4], 16)

            def load_w(f):
                if f >= 4:
                    sp.wait_ge(whi_done, f - 3)
                    sp.wait_ge(wlo_done, f - 3)
                sp.dma_start(stage[:, f % 4, :], wgu[f]).then_inc(stage_in[f % 4], 16)

            for pair in range(4):
                load_toep(pair)
            load_u(2)
            load_u(3)
            for pair in range(4, PAIRS):
                load_toep(pair)
                if pair == 7:
                    load_w(0)
                if pair == 11:
                    sp.dma_start(b2_raw[:, :], b2).then_inc(b2_in, 16)
                    load_w(1)
            load_we(7)
            load_w(2)
            load_w(3)
            sp.dma_start(wd_raw[:, :, :], wd).then_inc(wd_in, 16)
            for f in range(4, F):
                load_w(f)
            sp.wait_ge(aw_out[0], 16 * (E // 2))
            sp.wait_ge(aw_out[1], 16 * (E // 2))
            for n in range(2):
                sp.dma_start(xn_sb[:, n, :], xn[n]).then_inc(xn_in[n], 16)

            def load_x(n, slot):
                sp.wait_ge(x1_done, n - 1)
                sp.dma_start(xn_sb[:, slot, :], xn[bass.ds(n, 1)].rearrange("o p d -> p (o d)")).then_inc(xn_in[slot], 16)

            def store(n, g):
                sp.wait_ge(out_ready, n + (1 + FREE))
                sp.dma_start(out[bass.ds(n, 1)].rearrange("o p d -> p (o d)"), x1[:, g, :]).then_inc(out_done[g], 16)

            with sp.Fori(0, NT - 1) as t:
                for k in range(G):
                    load_x(t * G + (k + 2), k % 2)
                for g in range(G):
                    store(t * G + g, g)
            for k in range(2):
                load_x((NT - 1) * G + k + 2, k)
            for g in range(G):
                store((NT - 1) * G + g, g)
            for g in range(G):
                sp.wait_ge(out_done[g], 16 * NT)

        def dve_route(dve, n, g, bank, wh_out):
            dve.wait_ge(z_done, n + (1 + FREE))
            dve.wait_ge(wh_done, n + FREE)
            dve.tensor_reduce(mx[:, g, :], bank[:, 0:E], AX_X, ALU.max).then_inc(route, 1)
            dve.wait_ge(route, n * 4 + 1)
            dve.scalar_tensor_tensor(out=cand[:, g, :], in0=bank[:, 0:E], scalar=mx[:, g, 0:1],
                                     in1=con[:, K_RANK:K_RANK + E], op0=ALU.is_ge, op1=ALU.mult).then_inc(route, 1)
            dve.wait_ge(route, n * 4 + 2)
            dve.tensor_reduce(first[:, g, :], cand[:, g, :], AX_X, ALU.max).then_inc(route, 1)
            dve.wait_ge(route, n * 4 + 3)
            dve.tensor_scalar(rw[:, g, :], cand[:, g, :], first[:, g, 0:1], mx[:, g, 0:1], ALU.is_equal, ALU.mult).then_inc(route, 1)
            dve.wait_ge(route, n * 4 + 4)
            dve.wait_ge(wht_ps, n + FREE if wh_out is wh else FREE)
            dve.tensor_tensor(wh_out[:, :].rearrange("p (e r) -> p e r", e=E), bank[:, E:Z].rearrange("p (e r) -> p e r", e=E),
                              rw[:, g, :].unsqueeze(2).to_broadcast([P, E, R]), ALU.mult).then_inc(wh_done, 1)

        def dve_layer1(dve, f, n0):
            if f % 2 == 1 and f // 2 < G:
                dve_route(dve, n0 + f // 2, f // 2, z_ps, wh)
            if f % 2 == 0 and 0 <= f // 2 - 1 < G:
                n = n0 + (f // 2 - 1)
                dve.wait_ge(wht_done, n + (1 + FREE))
                dve.wait_ge(o_done, n + FREE)
                dve.tensor_tensor(wht_lo[:, :], z_ps[:, 256:256 + P], wht_hi[:, :].bitcast(F32), ALU.subtract).then_inc(whtlo_done, 1)
            if f % 2 == 1 and 0 <= f // 2 - 1 < G:
                g = f // 2 - 1
                n = n0 + g
                dve.wait_ge(o_done, n + (1 + FREE))
                dve.tensor_tensor(x1[:, g, :], s_ps[:, :], x1[:, g, :], ALU.add).then_inc(out_ready, 1)

        def dve_end(dve, g, step):
            n = (NT - 1) * G + g
            if step == "x1":
                dve_x1(dve, NT - 1, g, True)
            if step == "z":
                dve_route(dve, n, g, down_ps[g], wh_end[:, g, :])
            if step == "wht":
                dve.wait_ge(wht_done, n + 1 + FREE)
                dve.tensor_tensor(wht_lo_end[:, g, :], down_ps[g][:, 256:256 + P], wht_hi_end[:, g, :].bitcast(F32),
                                  ALU.subtract).then_inc(whtlo_done, 1)
            if step == "out":
                dve.wait_ge(o_done, n + 1 + FREE)
                dve.tensor_tensor(x1[:, g, :], down_ps[g][:, :], x1[:, g, :], ALU.add).then_inc(out_ready, 1)

        def dve_split_w(dve, f):
            dve.wait_ge(whi_done, f + 1)
            dve.tensor_tensor(w_lo[:, f, :, :, :].rearrange("p g c k -> p (g c k)"), stage[:, f % 4, :],
                              w_hi[:, f, :, :, :].rearrange("p g c k -> p (g c k)").bitcast(F32), ALU.subtract).then_inc(wlo_done, 1)

        def dve_split_y(dve, t):
            for i in range(C):
                dve.wait_ge(yhi_done, t * C + i + 1)
                dve.tensor_tensor(y_lo[:, i, :].rearrange("p (b h) -> p b h", h=H),
                                  uy[:, :, i, bass.ds(t * BT, BT)].rearrange("p h b -> p b h"),
                                  y_hi[:, i, :].rearrange("p (b h) -> p b h", h=H).bitcast(F32), ALU.subtract).then_inc(ylo_done, 1)

        def dve_tile(dve, t, first_tile):
            for f in range(F):
                n = t * F + f
                dve.wait_ge(silu_done, n + 1)
                dve.wait_ge(up_done, n + 1)
                if not (first_tile and f == 0):
                    dve.wait_ge(hhi_done, n)
                    dve.wait_ge(hlo_done, n)
                dve.tensor_tensor(prod_sb[:, :], gate_sb[:, :], up_ps[:, :], ALU.mult).then_inc(prod_done, 1)
                dve.wait_ge(wdhi_done, n + 1)
                dve.tensor_tensor(wd_lo[:, f % 2, :], wd_raw[:, f, :], wd_hi[:, f % 2, :].bitcast(F32), ALU.subtract).then_inc(wdlo_done, 1)
                dve.wait_ge(hhi_done, n + 1)
                dve.tensor_tensor(h_lo[:, f % 2, :], prod_sb[:, :], h_hi[:, f % 2, :].bitcast(F32), ALU.subtract).then_inc(hlo_done, 1)
                if first_tile and f + 2 < F:
                    dve_split_w(dve, f + 2)
                if not first_tile:
                    dve_layer1(dve, f, t * G - G)

        def dve_x1(dve, t, g, late):
            if late:
                dve.wait_ge(end_down, g + 1)
            else:
                dve.wait_ge(down_done, t * F + F)
            dve.wait_ge(xn_in[g % 2], t * (8 * G) + 16 * (g // 2 + 1))
            if not (isinstance(t, int) and t == 0):
                dve.wait_ge(out_done[g], t * 16)
            dve.tensor_tensor(x1[:, g, :], down_ps[g][:, :], xn_sb[:, g % 2, :], ALU.add).then_inc(x1_done, 1)

        def dve_s4d(dve):
            count = {s4d: 0, s4d_em: 0}

            def step(chain, ins):
                count[chain] += 1
                ins.then_inc(chain, 1)

            def seen(chain):
                if count[chain]:
                    dve.wait_ge(chain, count[chain])

            def S(i, w=1):
                return small[:, i:i + w, :]

            def tt(chain, o, a, b, op, wait=True):
                if wait:
                    seen(chain)
                step(chain, dve.tensor_tensor(o, a, b, op))

            def ts(chain, o, a, s1, s2, op0, op1=ALU.bypass):
                seen(chain)
                step(chain, dve.tensor_scalar(o, a, s1, s2, op0, op1) if s2 is not None else dve.tensor_scalar(o, a, s1, None, op0))

            def stt(chain, o, a, s, b, op0, op1, wait=True):
                flat = "p a h -> p (a h)"
                if wait:
                    seen(chain)
                step(chain, dve.scalar_tensor_tensor(out=o.rearrange(flat), in0=a.rearrange(flat), scalar=s, in1=b.rearrange(flat),
                                                     op0=op0, op1=op1))

            def exp_parts(ch, x, c, t, k, p, s):
                ts(ch, c, x, -87.0, 88.7, ALU.max, ALU.min)
                yield
                ts(ch, k, c, LOG2E, ROUND, ALU.mult, ALU.add)
                yield
                ts(ch, k, k, ROUND, None, ALU.subtract)
                yield
                stt(ch, t, k, -LN2_HI, c, ALU.mult, ALU.add)
                ts(ch, s.bitcast(I32), k, 127.0, None, ALU.add)
                yield
                stt(ch, t, k, -LN2_LO, t, ALU.mult, ALU.add)
                yield
                fact = [1.0, 2.0, 6.0, 24.0, 120.0, 720.0, 5040.0, 40320.0]
                ts(ch, p, t, 1.0 / fact[7], None, ALU.mult)
                yield
                for m in range(6, -1, -1):
                    stt(ch, p, p, 1.0 / fact[m], t, ALU.add, ALU.mult)
                    yield
                ts(ch, s.bitcast(I32), s.bitcast(I32), 23, None, ALU.logical_shift_left)
                yield

            dve.wait_ge(par_in, 16)
            for _ in exp_parts(s4d, par[:, 0:2, :], S(14, 2), S(0, 2), S(2, 2), S(4, 2), S(6, 2)):
                pass
            stt(s4d, S(4, 2), S(4, 2), 1.0, S(6, 2), ALU.add, ALU.mult)
            dt, ar, ai = S(4), S(5), par[:, 2:3, :]
            al, w_ = S(8), S(9)
            stt(s4d, al, ar, -1.0, dt, ALU.mult, ALU.mult)
            tt(s4d, w_, ai, dt, ALU.mult, wait=False)
            ts(s4d, S(13), al, float(NB), None, ALU.mult)
            s4d_at["exponent"] = count[s4d]

            def side():
                yield from exp_parts(s4d_em, al, S(21), S(22), S(23), S(24), S(25))
                tt(s4d_em, S(24), S(24), S(25), ALU.mult)
                yield
                ts(s4d_em, S(25), S(25), -1.0, None, ALU.add)
                yield
                tt(s4d_em, S(24), S(24), S(25), ALU.add)
                yield
                stt(s4d_em, S(28), ar, 0.5, ar, ALU.mult, ALU.mult, wait=False)
                stt(s4d_em, S(29), ai, 0.5, ai, ALU.mult, ALU.mult, wait=False)
                yield
                tt(s4d_em, S(28), S(28), S(29), ALU.add)
                yield
                seen(s4d_em)
                step(s4d_em, dve.reciprocal(S(28), S(28)))
                step(s4d_em, dve.tensor_scalar(par[:, 4:5, :], par[:, 4:5, :], con[:, K_SIGN:K_SIGN + 1], None, ALU.mult))
                yield

            em_steps = side()

            def em_step():
                next(em_steps, None)

            ts(s4d, S(10), w_, INV_2PI, None, ALU.mult)
            em_step()
            ts(s4d, S(11), S(10), ROUND, ROUND, ALU.add, ALU.subtract)
            em_step()
            tt(s4d, S(16), S(10), S(11), ALU.subtract)
            em_step()
            ts(s4d, S(12), S(16), 0.25, ROUND, ALU.add, ALU.add)
            em_step()
            ts(s4d, S(12), S(12), ROUND, -0.25, ALU.subtract, ALU.add)
            em_step()
            tt(s4d, S(17), S(16), S(12), ALU.subtract)
            s4d_at["angle"] = count[s4d]
            em_step()
            ts(s4d, S(10), S(16), float(NB), None, ALU.mult)
            em_step()
            ts(s4d, S(11), S(10), ROUND, ROUND, ALU.add, ALU.subtract)
            em_step()
            tt(s4d, S(15), S(10), S(11), ALU.subtract)
            em_step()
            dve.wait_ge(con_in, 64)
            tt(s4d, tab(phase, 1024, NB), over(16, NB), index(K_B, NB), ALU.mult)
            em_step()
            tt(s4d, tab(phase, 0, NA), over(15, NA), index(K_A, NA), ALU.mult, wait=False)
            em_step()
            ts(s4d, phase[:, 512:1024], phase[:, 0:512], 0.25, None, ALU.add)
            em_step()
            ts(s4d, phase[:, 1024:2048], phase[:, 1024:2048], con[:, K_OFF:K_OFF + 1], None, ALU.add)
            em_step()
            ts(s4d, whole[:, :], phase[:, :], ROUND, ROUND, ALU.add, ALU.subtract)
            em_step()
            tt(s4d, phase[:, :], phase[:, :], whole[:, :], ALU.subtract)
            s4d_at["turns"] = count[s4d]
            for _ in em_steps:
                pass
            seen(s4d_em)
            em, pair = S(24), "p a h -> p (a h)"
            dve.wait_ge(sin_done, 2)
            siny, cosy, sinh = S(18), S(19), S(20)
            tt(s4d, S(26), em, cosy, ALU.mult, wait=False)
            tt(s4d, S(30), sinh, sinh, ALU.mult, wait=False)
            stt(s4d, S(27), em, 1.0, siny, ALU.add, ALU.mult, wait=False)
            stt(s4d, S(26), S(30), -2.0, S(26), ALU.mult, ALU.add)
            def twice(i, w=1):
                return (small[:, i, :] if isinstance(i, int) else i).unsqueeze(1).to_broadcast([P, 2, H])

            tt(s4d, S(30, 2), S(26, 2), twice(5), ALU.mult)
            tt(s4d, S(32, 2), S(26, 2), twice(par[:, 2, :]), ALU.mult, wait=False)
            tt(s4d, S(34), S(33), S(30), ALU.subtract)
            tt(s4d, S(35), S(31), S(32), ALU.add, wait=False)
            tt(s4d, S(34, 2), S(34, 2), twice(28), ALU.mult)
            tt(s4d, S(30, 2), S(34, 2), twice(par[:, 3, :]), ALU.mult)
            tt(s4d, S(32, 2), S(34, 2), twice(par[:, 4, :]), ALU.mult, wait=False)
            tt(s4d, S(26), S(30), S(33), ALU.add)
            tt(s4d, S(27), S(31), S(32), ALU.subtract, wait=False)
            dve.wait_ge(sin_done, 3)
            tt(s4d, u_tab[:, :, :], tab(phase, 512, NA), over(26, NA), ALU.mult)
            tt(s4d, q_tab[:, :, :], tab(phase, 0, NA), over(27, NA), ALU.mult, wait=False)
            tt(s4d, u_tab[:, :, :], u_tab[:, :, :], q_tab[:, :, :], ALU.add)
            dve.wait_ge(exp_done, 1)
            seen(s4d)
            dve.tensor_tensor(u_tab[:, :, :], u_tab[:, :, :], tab(expo, 0, NA), ALU.mult).then_inc(u_done, 1)

        @block.vector
        def _(dve):
            dve.sem_inc(wh_done, FREE)
            dve.sem_inc(out_ready, FREE)
            dve.sem_inc(whtlo_done, FREE)
            dve_s4d(dve)
            for i in range(C):
                last = dve.tensor_scalar(mask[:, i, :], len_sb[:, :], con[:, K_L + i:K_L + i + 1], None, ALU.is_gt)
            last.then_inc(mask_done, 1)
            dve.tensor_scalar(id_neg, id_sb[:, :], 0.0, float(E), ALU.is_lt, ALU.mult).then_inc(mask_done, 1)
            dve.wait_ge(mask_done, 2)
            dve.tensor_tensor(id_fit, id_sb[:, :], id_neg, ALU.add).then_inc(mask_done, 1)
            dve.wait_ge(mask_done, 3)
            dve.tensor_scalar(id_row[:, :], id_fit, 0.0, float(E - 1), ALU.max, ALU.min).then_inc(ids_done, 1)
            dve.memset(zero[:, :], 0.0).then_inc(k_ready, 1)
            dve.wait_ge(k_done, 1)
            for i in range(2):
                last = dve.tensor_copy(k_sb[:, i * (H // 2):(i + 1) * (H // 2), :].rearrange("a h b -> a (h b)"), k_ps[i][0:NA, :])
            last.then_inc(mask_done, 1)
            dve.wait_ge(mask_done, 4)
            dve.tensor_tensor(k_sb[0:1, :, 0], k_sb[0:1, :, 0], dk_sb[:, :], ALU.add).then_inc(k_ready, 1)
            def mask_y(pair, s):
                dve.wait_ge(conv_done, pair + 1)
                dve.tensor_tensor(uy[:, bass.ds(pair * 2, 2), :, :].rearrange("p h c b -> p h (c b)"),
                                  down_ps[s][:, :].rearrange("p (h k) -> p h k", h=2),
                                  mask[:, :, :].rearrange("p c b -> p (c b)").unsqueeze(1).to_broadcast([P, 2, C * B]),
                                  ALU.mult).then_inc(y_done, 1)

            with dve.Fori(0, PAIRS // 4 - 1) as i:
                for s in range(4):
                    mask_y(i * 4 + s, s)
            dve_split_w(dve, 0)
            mask_y(PAIRS - 4, 0)
            dve.wait_ge(b2hi_done, 1)
            dve.tensor_tensor(b2_lo[:, :], b2_raw[:, :], b2_hi[:, :].bitcast(F32), ALU.subtract).then_inc(b2lo_done, 1)
            mask_y(PAIRS - 3, 1)
            dve_split_w(dve, 1)
            mask_y(PAIRS - 2, 2)
            mask_y(PAIRS - 1, 3)
            dve.wait_ge(y_done, PAIRS)
            dve_split_y(dve, 0)
            dve_tile(dve, 0, True)
            dve_split_y(dve, 1)
            for g in range(G):
                dve_x1(dve, 0, g, False)
            with dve.Fori(1, NT - 1) as t:
                dve_tile(dve, t, False)
                dve_split_y(dve, t + 1)
                for g in range(G):
                    dve_x1(dve, t, g, False)
            dve_tile(dve, NT - 1, False)
            for g, step in END_ORDER:
                dve_end(dve, g, step)

        def act_layer1(act, f, n0):
            if f % 2 == 0 and f // 2 < G:
                n = n0 + f // 2
                act.wait_ge(x1t_ps, n + 1)
                act.wait_ge(z_done, n + FREE)
                act.activation(x1t[:, :, :], s_ps[:, :].rearrange("p (c t) -> p c t", c=C), ACT.Copy).then_inc(x1t_done, 1)
            if f % 2 == 0 and 0 <= f // 2 - 1 < G:
                n = n0 + (f // 2 - 1)
                act.wait_ge(wht_ps, n + (1 + FREE))
                act.wait_ge(o_done, n + FREE)
                act.activation(wht_hi[:, :], z_ps[:, 256:256 + P], ACT.Copy).then_inc(wht_done, 1)

        def act_end(act, g, step):
            n = (NT - 1) * G + g
            if step == "x1t":
                act.wait_ge(x1t_ps, n + 1)
                act.activation(x1t_end[:, g, :, :], end_ps[g][:, :].rearrange("p (c t) -> p c t", c=C), ACT.Copy).then_inc(x1t_done, 1)
            else:
                act.wait_ge(wht_ps, n + 1 + FREE)
                act.activation(wht_hi_end[:, g, :], down_ps[g][:, 256:256 + P], ACT.Copy).then_inc(wht_done, 1)

        def act_split_w(act, f):
            act.wait_ge(stage_in[f % 4], 16 * (f // 4 + 1))
            act.activation(w_hi[:, f, :, :, :].rearrange("p g c k -> p (g c k)"), stage[:, f % 4, :], ACT.Copy).then_inc(whi_done, 1)

        def act_split_y(act, t):
            for i in range(C):
                act.activation(y_hi[:, i, :].rearrange("p (b h) -> p b h", h=H),
                               uy[:, :, i, bass.ds(t * BT, BT)].rearrange("p h b -> p b h"), ACT.Copy).then_inc(yhi_done, 1)

        def act_tile(act, t, first_tile):
            for f in range(F):
                n = t * F + f
                act.wait_ge(gate_done, n + 1)
                if not (first_tile and f == 0):
                    act.wait_ge(prod_done, n)
                act.activation(gate_sb[:, :], gate_ps[:, :], ACT.Silu).then_inc(silu_done, 1)
                if first_tile and f + 2 < F:
                    act_split_w(act, f + 2)
                if not (first_tile and f < 2):
                    act.wait_ge(down_done, n - 1 if f else n)
                act.activation(wd_hi[:, f % 2, :], wd_raw[:, f, :], ACT.Copy).then_inc(wdhi_done, 1)
                act.wait_ge(prod_done, n + 1)
                act.activation(h_hi[:, f % 2, :], prod_sb[:, :], ACT.Copy).then_inc(hhi_done, 1)
                if not first_tile:
                    act_layer1(act, f, t * G - G)

        @block.scalar
        def _(act):
            act.sem_inc(wht_done, FREE)
            act.wait_ge(s4d, s4d_at["angle"])
            act.activation(small[:, 18:20, :], small[:, 16:18, :], ACT.Sin, scale=TWO_PI).then_inc(sin_done, 1)
            act.activation(small[:, 20, :], small[:, 16, :], ACT.Sin, scale=TWO_PI / 2).then_inc(sin_done, 1)
            act.wait_ge(s4d, s4d_at["turns"])
            act.activation(phase[:, :], phase[:, :], ACT.Sin, scale=TWO_PI).then_inc(sin_done, 1)
            act.wait_ge(expo_done, 2)
            act.activation(expo[:, :], expo[:, :], ACT.Exp).then_inc(exp_done, 1)

            def copy_aw(e, s, peeled):
                act.wait_ge(aw_done, e + 1)
                if not peeled:
                    act.wait_ge(aw_out[s], e * 8 - 8 * s)
                for k in range(2):
                    last = act.activation(aw_sb[:, s, 2 * k:2 * k + 2, :].rearrange("p c z -> p (c z)"),
                                          aw_ps[s][k][:, 0:2 * Z], ACT.Copy)
                last.then_inc(aw_copied, 1)
                act.wait_ge(aw_copied, e + 1)
                act.dma_start(aw_dram[:, bass.ds(e * (C * Z), C * Z)],
                              aw_sb[:, s, :, :].rearrange("p c z -> p (c z)")).then_inc(aw_out[s], 16)

            for e in range(2):
                copy_aw(e, e, True)
            with act.Fori(1, E // 2 - 1) as i:
                for s in range(2):
                    copy_aw(i * 2 + s, s, False)
            copy_aw(E - 2, 0, False)
            act_split_w(act, 0)
            act.wait_ge(b2_in, 16)
            act.activation(b2_hi[:, :], b2_raw[:, :], ACT.Copy).then_inc(b2hi_done, 1)
            act_split_w(act, 1)
            act.wait_ge(y_done, PAIRS)
            act.wait_ge(conv_done, PAIRS)
            act_split_y(act, 0)
            copy_aw(E - 1, 1, False)
            act.wait_ge(wd_in, 16)

            def next_y(t):
                act.wait_ge(up_done, t * F + F)
                act_split_y(act, t + 1)

            act_tile(act, 0, True)
            next_y(0)
            with act.Fori(1, NT - 1) as t:
                act_tile(act, t, False)
                next_y(t)
            act_tile(act, NT - 1, False)
            for g, step in END_ORDER:
                if step in ("x1t", "wht"):
                    act_end(act, g, step)

        @block.gpsimd
        def _(pool):
            pool.wait_ge(con_in, 64)
            pool.wait_ge(s4d, s4d_at["exponent"])
            pool.tensor_tensor(tab(expo, 0, NA), over(13, NA), index(K_A, NA), ALU.mult).then_inc(expo_done, 1)
            pool.tensor_tensor(tab(expo, 512, NB), over(8, NB), index(K_B, NB), ALU.mult).then_inc(expo_done, 1)
            pool.wait_ge(sin_done, 3)
            pool.wait_ge(exp_done, 1)
            pool.tensor_tensor(v_tab[:, :, :], tab(phase, 1024, NB), tab(expo, 512, NB), ALU.mult).then_inc(v_done, 1)
            pool.wait_ge(ids_done, 1)
            pool.wait_ge(wlo_done, F)
            pool.wait_ge(whi_done, F)
            for s in range(2):
                pool.wait_ge(aw_out[s], 16 * (E // 2))

            def gather(b, j, slot):
                e = pool.value_load(id_row[0:1, bass.ds(b, 1)], min_val=0, max_val=E - 1)
                pool.dma_start(slot, aw_dram[:, bass.ds(e * (C * Z), C * Z)].rearrange("p (c z) -> p c z", c=C)).then_inc(mb_in[j], 16)

            END = TOK // P - G
            for j in range(GB):
                gather(j, j, mb[:, j, :, :])
            with pool.Fori(1, END + 1) as g:
                pool.wait_ge(z_done, g + FREE)
                for j in range(GB):
                    gather(g * GB + j, j, mb[:, j, :, :])
            pool.wait_ge(yhi_done, NT * C)
            pool.wait_ge(ylo_done, NT * C)
            for k in range(G - 1):
                for j in range(GB):
                    pool.wait_ge(mb_in[j], (END + k + 1) * 16)
                    gather((END + 1 + k) * GB + j, j, mb_end[:, k, j, :, :])

        def pe_transposes(pe, n, g, bank):
            pe.wait_ge(x1_done, n + 1)
            for c in range(C):
                last = pe.transpose(bank[:, c * P:(c + 1) * P], x1[:, g, c * P:(c + 1) * P], ident)
            last.then_inc(x1t_ps, 1)

        def pe_z(pe, n, bank, x1t_in, mb_in_sb):
            pe.wait_ge(x1t_done, n + 1)
            for j in range(GB):
                pe.wait_ge(mb_in[j], n * 16 + 16)
            for c in range(C):
                for j in range(GB):
                    last = pe.matmul(bank[H * j:H * j + H, 0:Z], x1t_in[:, c, H * j:H * j + H], mb_in_sb[:, j, c, :],
                                     start=(c == 0), stop=(c == C - 1), tile_position=(0, H * j))
            last.then_inc(z_done, 1)

        def pe_out(pe, n, bank, hi, lo):
            pe.wait_ge(whtlo_done, n + (1 + FREE))
            pe.matmul(bank[:, :], hi, b2_hi[:, :], start=True, stop=False)
            pe.matmul(bank[:, :], hi, b2_lo[:, :], start=False, stop=False)
            pe.matmul(bank[:, :], lo, b2_hi[:, :], start=False, stop=True).then_inc(o_done, 1)

        def pe_layer1(pe, f, n0):
            if f % 2 == 0 and f // 2 < G:
                g = f // 2
                n = n0 + g
                pe.wait_ge(out_ready, (n - 1 if g else n) + FREE)
                pe_transposes(pe, n, g, s_ps)
            if f % 2 == 0 and 0 <= f // 2 - 1 < G:
                n = n0 + (f // 2 - 1)
                pe.wait_ge(wh_done, n + (1 + FREE))
                pe.transpose(z_ps[:, 256:256 + P], wh[:, :], ident).then_inc(wht_ps, 1)
            if f % 2 == 1 and f // 2 < G:
                n = n0 + f // 2
                pe.wait_ge(wht_done, n + FREE)
                pe.wait_ge(whtlo_done, n + FREE)
                pe_z(pe, n, z_ps, x1t, mb)
            if f % 2 == 1 and 0 <= f // 2 - 1 < G:
                n = n0 + (f // 2 - 1)
                pe.wait_ge(x1t_done, n + (2 if f // 2 < G else 1))
                pe.wait_ge(out_ready, n + FREE)
                pe_out(pe, n, s_ps, wht_hi[:, :], wht_lo[:, :])

        def pe_end(pe, g, step):
            n = (NT - 1) * G + g
            if step == "down":
                for f in range(F - 2, F):
                    pe_down_group(pe, NT * F - F + f, f, g)
            if step == "x1t":
                if g == 2:
                    pe.wait_ge(out_ready, (NT - 1) * G + FREE)
                if g == 3:
                    pe.wait_ge(whtlo_done, (NT - 1) * G + FREE)
                pe_transposes(pe, n, g, end_ps[g])
            if step == "z":
                pe_z(pe, n, down_ps[g], x1t_end[:, g, :, :], mb if g == 0 else mb_end[:, g - 1, :, :, :])
            if step == "wht":
                pe.wait_ge(wh_done, n + 1 + FREE)
                pe.transpose(down_ps[g][:, 256:256 + P], wh_end[:, g, :], ident).then_inc(wht_ps, 1)
            if step == "out":
                pe_out(pe, n, down_ps[g], wht_hi_end[:, g, :], wht_lo_end[:, g, :])

        def pe_gate_up(pe, bank, f, k, y_from=None):
            for c in range(C):
                if y_from is not None:
                    pe.wait_ge(yhi_done, y_from + (c + 1))
                    pe.wait_ge(ylo_done, y_from + (c + 1))
                pe.matmul(bank[:, :], w_hi[:, f, k, c, :], y_hi[:, c, :], start=(c == 0), stop=False)
                pe.matmul(bank[:, :], w_hi[:, f, k, c, :], y_lo[:, c, :], start=False, stop=False)
                last = pe.matmul(bank[:, :], w_lo[:, f, k, c, :], y_hi[:, c, :], start=False, stop=(c == C - 1))
            return last

        def pe_down_group(pe, n, f, g):
            pe.wait_ge(wdlo_done, n + 1)
            pe.wait_ge(hlo_done, n + 1)
            tok = slice(g * P, (g + 1) * P)
            pe.matmul(down_ps[g][:, :], h_hi[:, f % 2, tok], wd_hi[:, f % 2, :], start=(f == 0), stop=False)
            pe.matmul(down_ps[g][:, :], h_hi[:, f % 2, tok], wd_lo[:, f % 2, :], start=False, stop=False)
            last = pe.matmul(down_ps[g][:, :], h_lo[:, f % 2, tok], wd_hi[:, f % 2, :], start=False, stop=(f == F - 1))
            if f == F - 1 and isinstance(n, int) and n == NT * F - 1:
                last.then_inc(end_down, 1)
            return last

        def pe_down(pe, n, f):
            for g in range(G):
                last = pe_down_group(pe, n, f, g)
            last.then_inc(down_done, 1)

        def pe_tile(pe, t, first_tile, last_tile=False):
            for f in range(F):
                n = t * F + f
                if first_tile:
                    pe.wait_ge(whi_done, f + 1)
                    pe.wait_ge(wlo_done, f + 1)
                if not (first_tile and f == 0):
                    pe.wait_ge(silu_done, n)
                pe_gate_up(pe, gate_ps, f, 0, t * C if f == 0 else None).then_inc(gate_done, 1)
                if not (first_tile and f == 0):
                    pe.wait_ge(prod_done, n)
                pe_gate_up(pe, up_ps, f, 1).then_inc(up_done, 1)
                if f == 1 and not first_tile:
                    pe.wait_ge(x1_done, t * G)
                if f and not (last_tile and f == F - 1):
                    pe_down(pe, n - 1, f - 1)
                if not first_tile:
                    pe_layer1(pe, f, t * G - G)
            if not last_tile:
                pe_down(pe, t * F + (F - 1), F - 1)

        @block.tensor
        def _(pe):
            pe.sem_inc(z_done, FREE)
            pe.sem_inc(wht_ps, FREE)
            pe.sem_inc(o_done, FREE)

            def aw(e):
                if e:
                    pe.wait_ge(we_in[e % 4], 16 * (e // 4 + (e % 4 > 0)))
                if e >= 2:
                    pe.wait_ge(aw_copied, e - 1)
                for ic in range(C):
                    if e == 0 and ic % 2 == 0:
                        pe.wait_ge(we_half[ic // 2], 16)
                    for oc in range(C):
                        last = pe.matmul(aw_ps[e % 2][ic // 2][:, (ic % 2) * Z:(ic % 2 + 1) * Z], we_sb[:, e % 4, oc, ic * P:(ic + 1) * P],
                                         ra_sb[:, oc, :], start=(oc == 0), stop=(oc == C - 1))
                last.then_inc(aw_done, 1)

            pe.wait_ge(ra_in, 16)
            for e in range(5):
                aw(e)
            pe.wait_ge(u_done, 1)
            pe.wait_ge(v_done, 1)
            for h in range(H):
                bank = k_ps[h // (H // 2)]
                col = (h % (H // 2)) * NB
                last = pe.matmul(bank[0:NA, col:col + NB], u_tab[:, h, :], v_tab[:, h, :], start=True, stop=True)
            last.then_inc(k_done, 1)
            aw(5)
            aw(6)
            pe.wait_ge(ut_in[0], 16)
            pe.wait_ge(k_ready, 2)

            def conv(pair, s, peeled):
                pe.wait_ge(toep_in[s], (pair - s) * 4 + 16)
                if not peeled:
                    pe.wait_ge(y_done, pair - 3)
                for k in range(2):
                    for d in range(C):
                        last = pe.matmul(down_ps[s][:, k * C * B + d * B:(k + 1) * C * B], toep[:, s, k, d * P:(d + 1) * P],
                                         uy[:, bass.ds(pair * 2 + k, 1), 0:C - d, :].rearrange("p h c b -> p (h c b)"),
                                         start=(k == 0 and d == 0), stop=(d == C - 1), skip_group_check=True)
                last.then_inc(conv_done, 1)

            for s in range(4):
                conv(s, s, True)
            for q in range(1, 4):
                pe.wait_ge(ut_in[q], 16)
            with pe.Fori(1, PAIRS // 4) as i:
                for s in range(4):
                    conv(i * 4 + s, s, False)
            aw(7)
            pe_tile(pe, 0, True)
            with pe.Fori(1, NT - 1) as t:
                pe_tile(pe, t, False)
            pe.wait_ge(b2lo_done, 1)
            pe_tile(pe, NT - 1, False, last_tile=True)
            for g, step in END_ORDER:
                pe_end(pe, g, step)


def kernel(**inputs):
    import numpy as np
    import concourse.bacc as bacc
    from concourse.bass_utils import run_bass_kernel_spmd

    def a(name):
        return np.asarray(inputs[name])

    x = a("x")
    ut = x.reshape(B, H, C, P)[:, :, :, ::-1].transpose(3, 1, 2, 0)

    def pad(w):
        return np.pad(w, ((0, F * P - D_FF), (0, 0)))

    wgu = np.stack([pad(a(n)).reshape(F, P, C, P).transpose(0, 3, 2, 1) for n in ("L0_ffn_W_gate", "L0_ffn_W_up")], 2)
    wd = pad(a("L0_ffn_W_down").T).reshape(F, P, L).transpose(1, 0, 2)
    we = a("L1_cond_weight").reshape(E, C, P, L).transpose(0, 2, 1, 3)
    ra = np.concatenate([a("L1_ffn_route_w"), a("L1_ffn_A").reshape(ER, L)]).T.reshape(C, P, Z).transpose(1, 0, 2)
    b2 = a("L1_ffn_Bw").transpose(0, 2, 1).reshape(ER, L)
    re, im = a("L0_cond_C")[..., 0].T, a("L0_cond_C")[..., 1].T

    def twice(m):
        return np.concatenate([m, m])

    params = np.stack([np.broadcast_to(a("L0_cond_log_dt"), (P, H)), twice(a("L0_cond_log_A_real").T), twice(a("L0_cond_A_imag").T),
                       np.concatenate([re, im]), np.concatenate([im, re])], 1)
    consts = np.zeros((P, K_END), np.float32)
    consts[:, K_ID:K_ID + P] = np.eye(P)
    consts[:, K_A:K_A + NA] = np.arange(NA)
    consts[:, K_B:K_B + NB] = np.arange(NB)
    consts[:, K_L:K_L + C] = np.arange(L).reshape(C, P).T
    consts[:, K_SIGN] = np.repeat([1, -1], N_STATE)
    consts[:, K_OFF] = np.repeat([0.25, 0.5], N_STATE)
    consts[:, K_RANK:K_RANK + E] = E - np.arange(E)
    arrays = {
        "params": params, "consts": consts, "d_skip": a("L0_cond_D").reshape(1, H),
        "lens": np.broadcast_to(a("itok_B_8_3872"), (P, B)), "ids": a("itok_B_3_7").reshape(1, B),
        "ut": ut, "xn": x.reshape(TOK // P, P, L), "wgu": wgu.reshape(F, P, 2 * C * P), "wd": wd, "we": we, "ra": ra, "b2": b2,
    }
    nc = bacc.Bacc("TRN2", target_bir_lowering=False, num_devices=1)
    arrays = {k: np.ascontiguousarray(v) for k, v in arrays.items()}
    aps = {k: nc.dram_tensor(k, v.shape, mybir.dt.from_np(v.dtype), kind="ExternalInput").ap() for k, v in arrays.items()}
    out = nc.dram_tensor("out", (TOK // P, P, L), F32, kind="ExternalOutput").ap()
    build(nc, out=out, **aps)
    r = run_bass_kernel_spmd(nc, [arrays], core_ids=[0])
    return r.results[0]["out"].reshape(B, H, L)
```

```python
from contextlib import ExitStack

import concourse.bass as bass
from concourse import mybir

ALU = mybir.AluOpType
ACT = mybir.ActivationFunctionType
F32 = mybir.dt.float32
F32R = mybir.dt.float32r
I32 = mybir.dt.int32
AX_X = mybir.AxisListType.X

P = 128
B, H, L = 64, 32, 512
N_STATE = 64
D_FF = 1376
E, R = 8, 16
C = L // P
F = -(-D_FF // P)
ER = E * R
Z = E + ER
NA = 16
NB = L // NA
TOK = B * H
TILE = 512
NT = TOK // TILE
BT = TILE // H
G = TILE // P
HALF = TILE // 2
GB = P // H
PAIRS = H // 2
KROW = P + L

K_ID, K_A, K_B, K_L, K_SIGN, K_OFF, K_RANK, K_END = 0, 128, 144, 176, 180, 181, 182, 190

LOG2E = 1.4426950408889634
LN2_HI = 0.693359375
LN2_LO = -2.12194440054690583e-4
FREE = 1
IDLE_PRODUCTS = 9
ROUND = 12582912.0
INV_2PI = 0.15915494309189535
TWO_PI = 6.283185


def build(nc, params, consts, d_skip, lens, ids, ut, xt, wgu, wd, we, ra, b2, out):
    ctx = ExitStack()
    with ctx:
        at = [16512]

        def sb(name, shape, dt, off=None):
            size = 4
            for n in shape[1:]:
                size *= n
            if off is None:
                off, at[0] = at[0], at[0] + -(-size // 32) * 32
            return nc.alloc_sbuf_tensor_at(name, shape, dt, offset=off)

        def region(size):
            off, at[0] = at[0], at[0] + size
            return off

        def sem(name):
            return ctx.enter_context(nc.semaphore(name))

        def ps(name):
            return ctx.enter_context(nc.psum_tensor(name, [P, 512], F32))

        r_whi, r_wlo = region(F * 4096), region(F * 4096)
        r_wd, r_uy, r_y = region(F * 2048), region(H * 1024), region(16384)
        r_h, r_wds, r_gt = region(8192), region(8192), region(4096)
        WD_FIRST = 3
        AW_F = 6
        assert E * C * Z * 4 <= (F - AW_F) * 4096
        r_x1, r_mb = region(8192), region(GB * C * Z * 4)
        r_xt = region(6656)
        w_hi = sb("w_hi", [P, F, 2, C, P], F32R, r_whi)
        w_lo = sb("w_lo", [P, F, 2, C, P], F32R, r_wlo)
        wd_raw = sb("wd_raw", [P, F, L], F32, r_wd)
        uy = sb("uy", [P, H, C, B], F32, r_uy)
        y_hi = sb("y_hi", [P, C, TILE], F32R, r_y)
        y_lo = sb("y_lo", [P, C, TILE], F32R, r_y + 8192)
        h_hi = sb("h_hi", [P, 2, TILE], F32R, r_h)
        h_lo = sb("h_lo", [P, 2, TILE], F32R, r_h + 4096)
        wd_hi = sb("wd_hi", [P, 2, L], F32R, r_wds)
        wd_lo = sb("wd_lo", [P, 2, L], F32R, r_wds + 4096)
        gate_sb = sb("gate_sb", [P, TILE], F32, r_gt)
        prod_sb = sb("prod_sb", [P, TILE], F32, r_gt + 2048)
        x1 = sb("x1", [P, C, TILE], F32, r_x1)
        mb = sb("mb", [P, GB, C, Z], F32, r_mb)
        xt_sb = sb("xt_sb", [P, 2, TILE], F32, r_xt)
        wh = sb("wh", [P, 2, ER], F32, r_xt + 4096)
        wht_hi = sb("wht_hi", [P, TILE], F32R, r_xt)
        wht_lo = sb("wht_lo", [P, TILE], F32R, r_xt + 2048)
        b2_hi = sb("b2_hi", [P, L], F32R)
        b2_lo = sb("b2_lo", [P, L], F32R)
        con = sb("con", [P, K_END], F32)
        id_sb = sb("id_sb", [1, B], I32)
        id_row = sb("id_row", [1, B], I32)
        mx = sb("mx", [P, 2, 1], F32)
        best = sb("best", [P, 2, E], F32)
        cand = sb("cand", [P, 2, E], F32)
        first = sb("first", [P, 2, 1], F32)
        chosen = sb("chosen", [P, 2, E], F32)
        rw = sb("rw", [P, 2, E], F32)
        dk_sb = sb("dk_sb", [1, H], F32)
        toep = sb("toep", [P, 4, 2, L], F32, r_y)
        we_sb = sb("we_sb", [P, 4, C, L], F32, r_wlo + 3 * 4096)
        stage = sb("stage", [P, 4, 2 * C * P], F32, r_x1)
        aw_sb = sb("aw_sb", [P, E, C, Z], F32, r_whi + AW_F * 4096)
        ra_sb = sb("ra_sb", [P, C, Z], F32, r_xt)
        phase = sb("phase", [P, 2048], F32, r_wd)
        whole = sb("whole", [P, 2048], F32, r_wd + 8192)
        expo = sb("expo", [P, 1536], F32, r_wd + 16384)
        u_tab = sb("u_tab", [P, H, NA], F32, r_h)
        v_tab = sb("v_tab", [P, H, NB], F32, r_h + 2048)
        q_tab = sb("q_tab", [P, H, NA], F32, r_h + 6144)
        k_sb = sb("k_sb", [NA, H, NB], F32, r_gt)
        par = sb("par", [P, 5, H], F32, r_wds)
        small = sb("small", [P, 40, H], F32, r_wds + 640)
        b2_raw = sb("b2_raw", [P, L], F32, r_wds + 5760)
        len_sb = sb("len_sb", [P, B], I32, r_wds + 7808)
        mask = sb("mask", [P, C, B], F32, r_h + 6144)
        idle_sb = sb("idle_sb", [P, P], F32, r_mb)
        id_neg = small[0:1, 36:38, :].rearrange("p a h -> p (a h)")
        id_fit = small[0:1, 38:40, :].rearrange("p a h -> p (a h)")
        mb_end = sb("mb_end", [P, G - 1, GB, C, Z], F32, r_uy)
        xt_end = sb("xt_end", [P, 2, TILE], F32, r_uy + (G - 1) * GB * C * Z * 4)
        assert at[0] <= nc.sbuf_top
        zero = sb("zero", [H, P], F32, r_mb + GB * C * Z * 4 - 512)
        ident = con[:, K_ID:K_ID + P]

        gate_ps, up_ps = ps("gate_ps"), ps("up_ps")
        down_ps = [ps(f"down_ps{c}") for c in range(C)]
        s_ps, z_ps = ps("s_ps"), ps("z_ps")
        aw_ps = [[gate_ps, up_ps], [s_ps, z_ps]]
        k_ps = down_ps[0:2]

        k_dram = nc.dram_tensor("k_dram", [H, KROW], F32)
        aw_dram = nc.dram_tensor("aw_dram", [P, E * C * Z], F32)

        par_in, con_in, ra_in, b2_in = sem("par_in"), sem("con_in"), sem("ra_in"), sem("b2_in")
        wd_in = [sem(f"wd_in{i}") for i in range(2)]
        zeros_done = sem("zeros_done")
        rows_in, k_copied = sem("rows_in"), sem("k_copied")
        we_part = [sem(f"we_part{i}") for i in range(C)]
        we_half = [sem(f"we_half{i}") for i in range(2)]
        we_in = [sem(f"we_in{i}") for i in range(4)]
        ut_in = sem("ut_in")
        toep_in = [sem(f"toep_in{i}") for i in range(4)]
        stage_in = [sem(f"stage_in{i}") for i in range(4)]
        xt_in = [sem(f"xt_in{i}") for i in range(2)]
        xt_end_in = sem("xt_end_in")
        mb_in = [sem(f"mb_in{i}") for i in range(GB)]
        out_done, last_out = [sem(f"out_done{c}") for c in range(C)], sem("last_out")
        k_out, aw_out = sem("k_out"), sem("aw_out")
        s4d, s4d_em, sin_done, expo_done, exp_done = sem("s4d"), sem("s4d_em"), sem("sin_done"), sem("expo_done"), sem("exp_done")
        s4d_at = {}
        u_done, v_done = sem("u_done"), sem("v_done")
        k_done, k_ready, mask_done, ids_done = sem("k_done"), sem("k_ready"), sem("mask_done"), sem("ids_done")
        aw_done, aw_copied = sem("aw_done"), sem("aw_copied")
        conv_done, y_done = sem("conv_done"), sem("y_done")
        whi_done, wlo_done = sem("whi_done"), sem("wlo_done")
        yhi_done, ylo_done = sem("yhi_done"), sem("ylo_done")
        gate_done, up_done, down_done = sem("gate_done"), sem("up_done"), sem("down_done")
        silu_done, prod_done = sem("silu_done"), sem("prod_done")
        hhi_done, hlo_done, wdhi_done, wdlo_done = sem("hhi_done"), sem("hlo_done"), sem("wdhi_done"), sem("wdlo_done")
        x1_done = sem("x1_done")
        z_done, wh_done, wht_ps, wht_done = sem("z_done"), sem("wh_done"), sem("wht_ps"), sem("wht_done")
        whtlo_done, b2hi_done, b2lo_done, end_down = sem("whtlo_done"), sem("b2hi_done"), sem("b2lo_done"), sem("end_down")
        o_done, out_ready, route = sem("o_done"), sem("out_ready"), sem("route")

        def over(i, n):
            return small[:, i, :].unsqueeze(2).to_broadcast([P, H, n])

        def index(k, n):
            return con[:, k:k + n].unsqueeze(1).to_broadcast([P, H, n])

        def tab(t, at_, n):
            return t[:, at_:at_ + H * n].rearrange("p (h n) -> p h n", n=n)

        Z_SLOTS, ROUTE_SLOTS, WHT_SLOTS, SPLIT_SLOT, OUT_SLOTS = (1, 3, 4, 6), (3, 6), (4, 7), 7, (8, 8, 9, 9)
        END_ORDER = [("down", 0, 0), ("down", 0, 1), ("x1", 0, 0), ("x1", 0, 1), ("down", 1, 0), ("down", 1, 1),
                     ("x1", 1, 0), ("z", 0, 0), ("z", 0, 1), ("x1", 1, 1), ("route", 0, 0), ("z", 1, 0), ("z", 1, 1),
                     ("wht", 0, 0), ("route", 1, 0),
                     ("out", 0, 0), ("out", 0, 1), ("wht", 1, 0), ("out", 1, 0), ("out", 1, 1)]

        def end_bank(a, k):
            return down_ps[2 * a + k]

        block = ctx.enter_context(nc.Block())

        @block.sync
        def _(sp):
            sp.dma_start(par[:, :, :], params).then_inc(par_in, 16)
            sp.dma_start(ra_sb[:, :, :], ra).then_inc(ra_in, 16)
            for k in range(C):
                sp.dma_start(we_sb[:, 0, :, k * P:(k + 1) * P], we[0][:, :, k * P:(k + 1) * P]).then_inc(we_part[k], 16)
            sp.dma_start(con[:, :], consts).then_inc(con_in, 16)
            for k in range(2):
                cols = slice(k * L // 2, (k + 1) * L // 2)
                sp.dma_start(we_sb[:, 1, :, cols], we[1][:, :, cols]).then_inc(we_half[k], 16)
            for e in range(2, 4):
                sp.dma_start(we_sb[:, e, :, :], we[e]).then_inc(we_in[e], 16)
            sp.dma_start(dk_sb[:, :], d_skip).then_inc(rows_in, 16)
            sp.dma_start(len_sb[:, :], lens).then_inc(rows_in, 16)
            sp.dma_start(id_sb[:, :], ids).then_inc(rows_in, 16)

            def load_u(q):
                if q:
                    sp.wait_ge(ut_in, 16 * q)
                sp.dma_start(uy[:, 8 * q:8 * q + 8, :, :], ut[:, 8 * q:8 * q + 8]).then_inc(ut_in, 16)

            def load_we(e):
                sp.wait_ge(aw_done, e - 3)
                sp.dma_start(we_sb[:, e % 4, :, :], we[e]).then_inc(we_in[e % 4], 16)

            load_we(4)
            load_we(5)
            load_we(6)
            load_u(0)
            sp.wait_ge(k_ready, 2)
            sp.dma_start(k_dram[:, 0:P], zero[:, :]).then_inc(k_out, 16)
            sp.dma_start(k_dram[:, P:KROW].rearrange("h (a b) -> a h b", a=NA), k_sb[:, :, :]).then_inc(k_out, 16)
            sp.wait_ge(k_out, 32)

            def load_toep(pair):
                if pair >= 4:
                    sp.wait_ge(conv_done, pair - 3)
                sp.dma_start(toep[:, pair % 4, :, :],
                             bass.AP(k_dram, pair * 2 * KROW + 1, [[1, P], [KROW, 2], [1, L]])).then_inc(toep_in[pair % 4], 16)

            def load_w(f):
                if f >= 4:
                    sp.wait_ge(whi_done, f - 3)
                    sp.wait_ge(wlo_done, f - 3)
                sp.dma_start(stage[:, f % 4, :], wgu[f]).then_inc(stage_in[f % 4], 16)

            for pair in range(4):
                load_toep(pair)
            load_u(1)
            for pair in range(4, PAIRS):
                load_toep(pair)
                if pair in (5, 9):
                    load_u(pair // 4 + 1)
                if pair == 13:
                    load_w(0)
            sp.dma_start(b2_raw[:, :], b2).then_inc(b2_in, 16)
            load_w(1)
            load_we(7)
            load_w(2)
            load_w(3)
            sp.dma_start(wd_raw[:, 0:WD_FIRST, :], wd[:, 0:WD_FIRST]).then_inc(wd_in[0], 16)
            load_w(4)
            sp.dma_start(wd_raw[:, WD_FIRST:F, :], wd[:, WD_FIRST:F]).then_inc(wd_in[1], 16)
            load_w(5)
            sp.wait_ge(aw_copied, E)
            sp.dma_start(aw_dram[:, :], aw_sb[:, :, :, :].rearrange("p e c z -> p (e c z)")).then_inc(aw_out, 16)
            for f in range(6, F):
                load_w(f)
            sp.wait_ge(aw_done, E)
            for n in range(2):
                sp.dma_start(xt_sb[:, n, :], xt[n]).then_inc(xt_in[n], 16)
            with sp.Fori(0, NT - 1) as t:
                def load_x(k):
                    sp.dma_start(xt_sb[:, k % 2, :], xt[bass.ds(t * C + (k + 2), 1)].rearrange("o p d -> p (o d)")).then_inc(xt_in[k % 2], 16)

                for k in range(2):
                    sp.wait_ge(x1_done, t * C + (k + 1))
                    load_x(k)
                for c in range(C):
                    sp.wait_ge(out_ready, t * C + (c + 1 + FREE))
                    sp.dma_start(out[bass.ds(t * C + c, 1)].rearrange("o p d -> p (o d)"), x1[:, c, :]).then_inc(out_done[c], 16)
                for k in range(2, 4):
                    load_x(k)
            sp.wait_ge(yhi_done, NT * C)
            sp.wait_ge(ylo_done, NT * C)
            for k in range(2):
                sp.dma_start(xt_end[:, k, :], xt[(NT - 1) * C + 2 + k]).then_inc(xt_end_in, 16)
            last = NT * C - C
            for i in range(4):
                a, k = divmod(i, 2)
                sp.wait_ge(out_ready, last + i + 1 + FREE)
                sp.dma_start(out[last + 2 * k:last + 2 * k + 2, :, a * HALF:(a + 1) * HALF].rearrange("c p d -> p c d"),
                             x1[:, 2 * k:2 * k + 2, a * HALF:(a + 1) * HALF]).then_inc(last_out, 16)
            for c in range(C):
                sp.wait_ge(out_done[c], 16 * (NT - 1))
            sp.wait_ge(last_out, 16 * 4)

        def dve_route(dve, m, p, bank):
            n = m * 2 + p
            logits = bank[:, :].rearrange("p (i k) -> p i k", i=2)[:, :, 0:E]
            prods = bank[:, :].rearrange("p (i k) -> p i k", i=2)[:, :, E:Z].rearrange("p i (e r) -> p i e r", e=E)
            dve.wait_ge(z_done, m * G + (2 * p + 2))
            dve.wait_ge(wh_done, n + FREE)
            dve.tensor_reduce(mx[:, :, :], logits, AX_X, ALU.max).then_inc(route, 1)
            dve.wait_ge(route, n * 6 + 1)
            dve.tensor_tensor(best[:, :, :], logits, mx[:, :, :].to_broadcast([P, 2, E]), ALU.is_ge).then_inc(route, 1)
            dve.wait_ge(route, n * 6 + 2)
            dve.tensor_tensor(cand[:, :, :], best[:, :, :], con[:, K_RANK:K_RANK + E].unsqueeze(1).to_broadcast([P, 2, E]),
                              ALU.mult).then_inc(route, 1)
            dve.wait_ge(route, n * 6 + 3)
            dve.tensor_reduce(first[:, :, :], cand[:, :, :], AX_X, ALU.max).then_inc(route, 1)
            dve.wait_ge(route, n * 6 + 4)
            dve.tensor_tensor(chosen[:, :, :], cand[:, :, :], first[:, :, :].to_broadcast([P, 2, E]), ALU.is_equal).then_inc(route, 1)
            dve.wait_ge(route, n * 6 + 5)
            dve.tensor_tensor(rw[:, :, :], chosen[:, :, :], mx[:, :, :].to_broadcast([P, 2, E]), ALU.mult).then_inc(route, 1)
            dve.wait_ge(route, n * 6 + 6)
            dve.wait_ge(wht_ps, n + FREE)
            dve.tensor_tensor(wh[:, :, :].rearrange("p i (e r) -> p i e r", e=E), prods,
                              rw[:, :, :].unsqueeze(3).to_broadcast([P, 2, E, R]), ALU.mult).then_inc(wh_done, 1)

        def dve_layer1(dve, f, m):
            if f in ROUTE_SLOTS:
                dve_route(dve, m, ROUTE_SLOTS.index(f), z_ps)
            if f == SPLIT_SLOT:
                dve.wait_ge(wht_done, m + 1)
                dve.wait_ge(o_done, m * C + FREE)
                dve.tensor_tensor(wht_lo[:, :], s_ps[:, :], wht_hi[:, :].bitcast(F32), ALU.subtract).then_inc(whtlo_done, 1)
            for c in (c for c in range(C) if OUT_SLOTS[c] == f):
                dve.wait_ge(o_done, m * C + (c + 1 + FREE))
                dve.tensor_tensor(x1[:, c, :], [z_ps, s_ps][c % 2][:, :], x1[:, c, :], ALU.add).then_inc(out_ready, 1)

        def dve_end(dve, step, a, k):
            m = NT - 1
            tok, ds = slice(a * HALF, (a + 1) * HALF), slice(2 * k, 2 * k + 2)
            bank = end_bank(a, k)[:, :].rearrange("p (c t) -> p c t", c=2)
            if step == "x1":
                dve.wait_ge(end_down, 2 * a + k + 1)
                if k == 0:
                    for i in range(2):
                        dve.wait_ge(xt_in[i], 16 * (m * 2 + 1))
                else:
                    dve.wait_ge(xt_end_in, 32)
                for c in (2 * k, 2 * k + 1):
                    dve.wait_ge(out_done[c], 16 * m)
                dve.tensor_tensor(x1[:, ds, tok], bank, [xt_sb, xt_end][k][:, :, tok], ALU.add).then_inc(x1_done, 1)
            if step == "route":
                dve_route(dve, m, a, [gate_ps, up_ps][a])
            if step == "wht":
                dve.wait_ge(wht_done, m + a + 1)
                dve.wait_ge(o_done, m * C + FREE)
                dve.tensor_tensor(wht_lo[:, tok], [s_ps, z_ps][a][:, tok], wht_hi[:, tok].bitcast(F32), ALU.subtract).then_inc(whtlo_done, 1)
            if step == "out":
                dve.wait_ge(o_done, m * C + 2 * a + k + 1 + FREE)
                dve.tensor_tensor(x1[:, ds, tok], bank, x1[:, ds, tok], ALU.add).then_inc(out_ready, 1)

        def dve_split_w(dve, f):
            dve.wait_ge(whi_done, f + 1)
            dve.tensor_tensor(w_lo[:, f, :, :, :].rearrange("p g c k -> p (g c k)"), stage[:, f % 4, :],
                              w_hi[:, f, :, :, :].rearrange("p g c k -> p (g c k)").bitcast(F32), ALU.subtract).then_inc(wlo_done, 1)

        def dve_split_y(dve, t):
            for i in range(C):
                dve.wait_ge(yhi_done, t * C + i + 1)
                dve.tensor_tensor(y_lo[:, i, :].rearrange("p (b h) -> p b h", h=H),
                                  uy[:, :, i, bass.ds(t * BT, BT)].rearrange("p h b -> p b h"),
                                  y_hi[:, i, :].rearrange("p (b h) -> p b h", h=H).bitcast(F32), ALU.subtract).then_inc(ylo_done, 1)

        def dve_tile(dve, t, first_tile):
            for f in range(F):
                n = t * F + f
                dve.wait_ge(silu_done, n + 1)
                dve.wait_ge(up_done, n + 1)
                if not (first_tile and f == 0):
                    dve.wait_ge(hhi_done, n)
                    dve.wait_ge(hlo_done, n)
                dve.tensor_tensor(prod_sb[:, :], gate_sb[:, :], up_ps[:, :], ALU.mult).then_inc(prod_done, 1)
                dve.wait_ge(wdhi_done, n + 1)
                dve.tensor_tensor(wd_lo[:, f % 2, :], wd_raw[:, f, :], wd_hi[:, f % 2, :].bitcast(F32), ALU.subtract).then_inc(wdlo_done, 1)
                dve.wait_ge(hhi_done, n + 1)
                dve.tensor_tensor(h_lo[:, f % 2, :], prod_sb[:, :], h_hi[:, f % 2, :].bitcast(F32), ALU.subtract).then_inc(hlo_done, 1)
                if first_tile and f + 2 < F:
                    dve_split_w(dve, f + 2)
                if not first_tile:
                    dve_layer1(dve, f, t - 1)

        def dve_x1(dve, t, c):
            dve.wait_ge(down_done, t * F + F)
            dve.wait_ge(xt_in[c % 2], t * (8 * C) + 16 * (c // 2 + 1))
            if not (isinstance(t, int) and t == 0):
                dve.wait_ge(out_done[c], t * 16)
            dve.tensor_tensor(x1[:, c, :], down_ps[c][:, :], xt_sb[:, c % 2, :], ALU.add).then_inc(x1_done, 1)

        def dve_s4d(dve):
            count = {s4d: 0, s4d_em: 0}

            def step(chain, ins):
                count[chain] += 1
                ins.then_inc(chain, 1)

            def seen(chain):
                if count[chain]:
                    dve.wait_ge(chain, count[chain])

            def S(i, w=1):
                return small[:, i:i + w, :]

            def tt(chain, o, a, b, op, wait=True):
                if wait:
                    seen(chain)
                step(chain, dve.tensor_tensor(o, a, b, op))

            def ts(chain, o, a, s1, s2, op0, op1=ALU.bypass):
                seen(chain)
                step(chain, dve.tensor_scalar(o, a, s1, s2, op0, op1) if s2 is not None else dve.tensor_scalar(o, a, s1, None, op0))

            def stt(chain, o, a, s, b, op0, op1, wait=True):
                flat = "p a h -> p (a h)"
                if wait:
                    seen(chain)
                step(chain, dve.scalar_tensor_tensor(out=o.rearrange(flat), in0=a.rearrange(flat), scalar=s, in1=b.rearrange(flat),
                                                     op0=op0, op1=op1))

            def exp_parts(ch, x, c, t, k, p, s):
                ts(ch, c, x, -87.0, 88.7, ALU.max, ALU.min)
                yield
                ts(ch, k, c, LOG2E, ROUND, ALU.mult, ALU.add)
                yield
                ts(ch, k, k, ROUND, None, ALU.subtract)
                yield
                stt(ch, t, k, -LN2_HI, c, ALU.mult, ALU.add)
                ts(ch, s.bitcast(I32), k, 127.0, None, ALU.add)
                yield
                stt(ch, t, k, -LN2_LO, t, ALU.mult, ALU.add)
                yield
                fact = [1.0, 2.0, 6.0, 24.0, 120.0, 720.0, 5040.0, 40320.0]
                ts(ch, p, t, 1.0 / fact[7], None, ALU.mult)
                yield
                for m in range(6, -1, -1):
                    stt(ch, p, p, 1.0 / fact[m], t, ALU.add, ALU.mult)
                    yield
                ts(ch, s.bitcast(I32), s.bitcast(I32), 23, None, ALU.logical_shift_left)
                yield

            dve.wait_ge(par_in, 16)
            for _ in exp_parts(s4d, par[:, 0:2, :], S(14, 2), S(0, 2), S(2, 2), S(4, 2), S(6, 2)):
                pass
            stt(s4d, S(4, 2), S(4, 2), 1.0, S(6, 2), ALU.add, ALU.mult)
            dt, ar, ai = S(4), S(5), par[:, 2:3, :]
            al, wi = S(8), S(9)
            stt(s4d, al, ar, -1.0, dt, ALU.mult, ALU.mult)
            tt(s4d, wi, ai, dt, ALU.mult, wait=False)
            ts(s4d, S(13), al, float(NB), None, ALU.mult)
            s4d_at["exponent"] = count[s4d]

            def side():
                yield from exp_parts(s4d_em, al, S(21), S(22), S(23), S(24), S(25))
                tt(s4d_em, S(24), S(24), S(25), ALU.mult)
                yield
                ts(s4d_em, S(25), S(25), -1.0, None, ALU.add)
                yield
                tt(s4d_em, S(24), S(24), S(25), ALU.add)
                yield
                stt(s4d_em, S(28), ar, 0.5, ar, ALU.mult, ALU.mult, wait=False)
                stt(s4d_em, S(29), ai, 0.5, ai, ALU.mult, ALU.mult, wait=False)
                yield
                tt(s4d_em, S(28), S(28), S(29), ALU.add)
                yield
                seen(s4d_em)
                step(s4d_em, dve.reciprocal(S(28), S(28)))
                step(s4d_em, dve.tensor_scalar(par[:, 4:5, :], par[:, 4:5, :], con[:, K_SIGN:K_SIGN + 1], None, ALU.mult))
                yield

            em_steps = side()

            def em_step():
                next(em_steps, None)

            ts(s4d, S(10), wi, INV_2PI, None, ALU.mult)
            em_step()
            ts(s4d, S(11), S(10), ROUND, ROUND, ALU.add, ALU.subtract)
            em_step()
            tt(s4d, S(16), S(10), S(11), ALU.subtract)
            em_step()
            ts(s4d, S(12), S(16), 0.25, ROUND, ALU.add, ALU.add)
            em_step()
            ts(s4d, S(12), S(12), ROUND, -0.25, ALU.subtract, ALU.add)
            em_step()
            tt(s4d, S(17), S(16), S(12), ALU.subtract)
            s4d_at["angle"] = count[s4d]
            em_step()
            ts(s4d, S(10), S(16), float(NB), None, ALU.mult)
            em_step()
            ts(s4d, S(11), S(10), ROUND, ROUND, ALU.add, ALU.subtract)
            em_step()
            tt(s4d, S(15), S(10), S(11), ALU.subtract)
            em_step()
            dve.wait_ge(con_in, 16)
            tt(s4d, tab(phase, 1024, NB), over(16, NB), index(K_B, NB), ALU.mult)
            em_step()
            tt(s4d, tab(phase, 0, NA), over(15, NA), index(K_A, NA), ALU.mult, wait=False)
            em_step()
            ts(s4d, phase[:, 512:1024], phase[:, 0:512], 0.25, None, ALU.add)
            em_step()
            ts(s4d, phase[:, 1024:2048], phase[:, 1024:2048], con[:, K_OFF:K_OFF + 1], None, ALU.add)
            em_step()
            ts(s4d, whole[:, :], phase[:, :], ROUND, ROUND, ALU.add, ALU.subtract)
            em_step()
            tt(s4d, phase[:, :], phase[:, :], whole[:, :], ALU.subtract)
            s4d_at["turns"] = count[s4d]
            for _ in em_steps:
                pass
            seen(s4d_em)
            em, pair = S(24), "p a h -> p (a h)"
            dve.wait_ge(sin_done, 2)
            siny, cosy, sinh = S(18), S(19), S(20)
            tt(s4d, S(26), em, cosy, ALU.mult, wait=False)
            tt(s4d, S(30), sinh, sinh, ALU.mult, wait=False)
            stt(s4d, S(27), em, 1.0, siny, ALU.add, ALU.mult, wait=False)
            stt(s4d, S(26), S(30), -2.0, S(26), ALU.mult, ALU.add)
            def twice(i, w=1):
                return (small[:, i, :] if isinstance(i, int) else i).unsqueeze(1).to_broadcast([P, 2, H])

            tt(s4d, S(30, 2), S(26, 2), twice(5), ALU.mult)
            tt(s4d, S(32, 2), S(26, 2), twice(par[:, 2, :]), ALU.mult, wait=False)
            tt(s4d, S(34), S(33), S(30), ALU.subtract)
            tt(s4d, S(35), S(31), S(32), ALU.add, wait=False)
            tt(s4d, S(34, 2), S(34, 2), twice(28), ALU.mult)
            tt(s4d, S(30, 2), S(34, 2), twice(par[:, 3, :]), ALU.mult)
            tt(s4d, S(32, 2), S(34, 2), twice(par[:, 4, :]), ALU.mult, wait=False)
            tt(s4d, S(26), S(30), S(33), ALU.add)
            tt(s4d, S(27), S(31), S(32), ALU.subtract, wait=False)
            dve.wait_ge(sin_done, 3)
            tt(s4d, u_tab[:, :, :], tab(phase, 512, NA), over(26, NA), ALU.mult)
            tt(s4d, q_tab[:, :, :], tab(phase, 0, NA), over(27, NA), ALU.mult, wait=False)
            tt(s4d, u_tab[:, :, :], u_tab[:, :, :], q_tab[:, :, :], ALU.add)
            dve.wait_ge(exp_done, 1)
            seen(s4d)
            dve.tensor_tensor(u_tab[:, :, :], u_tab[:, :, :], tab(expo, 0, NA), ALU.mult).then_inc(u_done, 1)
            heads = slice(H // 2, H)
            dve.wait_ge(expo_done, 2)
            dve.tensor_tensor(v_tab[:, heads, :], tab(phase, 1024, NB)[:, heads, :], tab(expo, 512, NB)[:, heads, :],
                              ALU.mult).then_inc(v_done, 1)

        @block.vector
        def _(dve):
            dve.sem_inc(wh_done, FREE)
            dve.sem_inc(out_ready, FREE)
            dve.memset(idle_sb[:, :], 0.0).then_inc(zeros_done, 1)
            dve_s4d(dve)
            dve.wait_ge(rows_in, 48)
            for i in range(C):
                last = dve.tensor_scalar(mask[:, i, :], len_sb[:, :], con[:, K_L + i:K_L + i + 1], None, ALU.is_gt)
            last.then_inc(mask_done, 1)
            dve.tensor_scalar(id_neg, id_sb[:, :], 0.0, float(E), ALU.is_lt, ALU.mult).then_inc(mask_done, 1)
            dve.wait_ge(mask_done, 2)
            dve.tensor_tensor(id_fit, id_sb[:, :], id_neg, ALU.add).then_inc(mask_done, 1)
            dve.wait_ge(mask_done, 3)
            dve.tensor_scalar(id_row[:, :], id_fit, 0.0, float(E - 1), ALU.max, ALU.min).then_inc(ids_done, 1)
            dve.memset(zero[:, :], 0.0).then_inc(k_ready, 1)
            dve.wait_ge(k_done, 1)
            dve.tensor_copy(k_sb[:, 0:H // 2, :].rearrange("a h b -> a (h b)"), k_ps[0][0:NA, :]).then_inc(k_copied, 1)
            dve.wait_ge(k_copied, 2)
            dve.tensor_tensor(k_sb[0:1, :, 0], k_sb[0:1, :, 0], dk_sb[:, :], ALU.add).then_inc(k_ready, 1)
            def mask_y(pair, s):
                dve.wait_ge(conv_done, pair + 1)
                dve.tensor_tensor(uy[:, bass.ds(pair * 2, 2), :, :].rearrange("p h c b -> p h (c b)"),
                                  down_ps[s][:, :].rearrange("p (h k) -> p h k", h=2),
                                  mask[:, :, :].rearrange("p c b -> p (c b)").unsqueeze(1).to_broadcast([P, 2, C * B]),
                                  ALU.mult).then_inc(y_done, 1)

            with dve.Fori(0, PAIRS // 4 - 1) as i:
                for s in range(4):
                    mask_y(i * 4 + s, s)
            dve_split_w(dve, 0)
            mask_y(PAIRS - 4, 0)
            dve.wait_ge(b2hi_done, 1)
            dve.tensor_tensor(b2_lo[:, :], b2_raw[:, :], b2_hi[:, :].bitcast(F32), ALU.subtract).then_inc(b2lo_done, 1)
            mask_y(PAIRS - 3, 1)
            dve_split_w(dve, 1)
            mask_y(PAIRS - 2, 2)
            mask_y(PAIRS - 1, 3)
            dve.wait_ge(y_done, PAIRS)
            dve_split_y(dve, 0)
            dve_tile(dve, 0, True)
            dve_split_y(dve, 1)
            for c in range(C):
                dve_x1(dve, 0, c)
            with dve.Fori(1, NT - 1) as t:
                dve_tile(dve, t, False)
                dve_split_y(dve, t + 1)
                for c in range(C):
                    dve_x1(dve, t, c)
            dve_tile(dve, NT - 1, False)
            for step, a, k in END_ORDER:
                dve_end(dve, step, a, k)

        def act_wht(act, m, count, bank, tok):
            act.wait_ge(wht_ps, count + FREE)
            act.wait_ge(o_done, m * C + FREE)
            act.activation(wht_hi[:, tok], bank[:, tok], ACT.Copy).then_inc(wht_done, 1)

        def act_split_w(act, f):
            if f == AW_F:
                act.wait_ge(aw_out, 16)
            act.wait_ge(stage_in[f % 4], 16 * (f // 4 + 1))
            act.activation(w_hi[:, f, :, :, :].rearrange("p g c k -> p (g c k)"), stage[:, f % 4, :], ACT.Copy).then_inc(whi_done, 1)

        def act_split_y(act, t):
            for i in range(C):
                act.activation(y_hi[:, i, :].rearrange("p (b h) -> p b h", h=H),
                               uy[:, :, i, bass.ds(t * BT, BT)].rearrange("p h b -> p b h"), ACT.Copy).then_inc(yhi_done, 1)

        def act_tile(act, t, first_tile):
            for f in range(F):
                n = t * F + f
                act.wait_ge(gate_done, n + 1)
                if not (first_tile and f == 0):
                    act.wait_ge(prod_done, n)
                act.activation(gate_sb[:, :], gate_ps[:, :], ACT.Silu).then_inc(silu_done, 1)
                if first_tile and f + 2 < F:
                    act_split_w(act, f + 2)
                if first_tile and f in (0, WD_FIRST):
                    act.wait_ge(wd_in[f // WD_FIRST], 16)
                if not (first_tile and f < 2):
                    act.wait_ge(down_done, n - 1 if f else n)
                act.activation(wd_hi[:, f % 2, :], wd_raw[:, f, :], ACT.Copy).then_inc(wdhi_done, 1)
                act.wait_ge(prod_done, n + 1)
                act.activation(h_hi[:, f % 2, :], prod_sb[:, :], ACT.Copy).then_inc(hhi_done, 1)
                if f == SPLIT_SLOT and not first_tile:
                    act_wht(act, t - 1, t * 2, s_ps, slice(0, TILE))

        @block.scalar
        def _(act):
            act.wait_ge(s4d, s4d_at["angle"])
            act.activation(small[:, 18:20, :], small[:, 16:18, :], ACT.Sin, scale=TWO_PI).then_inc(sin_done, 1)
            act.activation(small[:, 20, :], small[:, 16, :], ACT.Sin, scale=TWO_PI / 2).then_inc(sin_done, 1)
            def copy_aw(e):
                act.wait_ge(aw_done, e + 1)
                for k in range(2):
                    last = act.activation(aw_sb[:, e, 2 * k:2 * k + 2, :].rearrange("p c z -> p (c z)"),
                                          aw_ps[e % 2][k][:, 0:2 * Z], ACT.Copy)
                last.then_inc(aw_copied, 1)

            copy_aw(0)
            copy_aw(1)
            act.wait_ge(s4d, s4d_at["turns"])
            act.activation(phase[:, :], phase[:, :], ACT.Sin, scale=TWO_PI).then_inc(sin_done, 1)
            copy_aw(2)
            act.wait_ge(expo_done, 2)
            act.activation(expo[:, :], expo[:, :], ACT.Exp).then_inc(exp_done, 1)
            for e in range(3, 5):
                copy_aw(e)
            act.wait_ge(k_done, 1)
            act.activation(k_sb[:, H // 2:H, :].rearrange("a h b -> a (h b)"), k_ps[1][0:NA, :], ACT.Copy).then_inc(k_copied, 1)
            for e in range(5, E - 1):
                copy_aw(e)
            act_split_w(act, 0)
            act.wait_ge(b2_in, 16)
            act.activation(b2_hi[:, :], b2_raw[:, :], ACT.Copy).then_inc(b2hi_done, 1)
            act_split_w(act, 1)
            act.wait_ge(y_done, PAIRS)
            act.wait_ge(conv_done, PAIRS)
            act_split_y(act, 0)
            copy_aw(E - 1)

            def next_y(t):
                act.wait_ge(up_done, t * F + F)
                act_split_y(act, t + 1)

            act_tile(act, 0, True)
            next_y(0)
            with act.Fori(1, NT - 1) as t:
                act_tile(act, t, False)
                next_y(t)
            act_tile(act, NT - 1, False)
            for a in range(2):
                act_wht(act, NT - 1, (NT - 1) * 2 + a + 1, [s_ps, z_ps][a], slice(a * HALF, (a + 1) * HALF))

        @block.gpsimd
        def _(pool):
            pool.wait_ge(con_in, 16)
            pool.wait_ge(s4d, s4d_at["exponent"])
            pool.tensor_tensor(tab(expo, 0, NA), over(13, NA), index(K_A, NA), ALU.mult).then_inc(expo_done, 1)
            pool.tensor_tensor(tab(expo, 512, NB), over(8, NB), index(K_B, NB), ALU.mult).then_inc(expo_done, 1)
            pool.wait_ge(sin_done, 3)
            pool.wait_ge(exp_done, 1)
            heads = slice(0, H // 2)
            pool.tensor_tensor(v_tab[:, heads, :], tab(phase, 1024, NB)[:, heads, :], tab(expo, 512, NB)[:, heads, :],
                               ALU.mult).then_inc(v_done, 1)
            pool.wait_ge(ids_done, 1)
            pool.wait_ge(wlo_done, F)
            pool.wait_ge(whi_done, F)
            pool.wait_ge(aw_out, 16)

            def gather(b, j, slot):
                e = pool.value_load(id_row[0:1, bass.ds(b, 1)], min_val=0, max_val=E - 1)
                pool.dma_start(slot, aw_dram[:, bass.ds(e * (C * Z), C * Z)].rearrange("p (c z) -> p c z", c=C)).then_inc(mb_in[j], 16)

            END = TOK // P - G
            for j in range(GB):
                gather(j, j, mb[:, j, :, :])
            with pool.Fori(1, END + 1) as g:
                pool.wait_ge(z_done, g)
                for j in range(GB):
                    gather(g * GB + j, j, mb[:, j, :, :])
            pool.wait_ge(yhi_done, NT * C)
            pool.wait_ge(ylo_done, NT * C)
            for k in range(G - 1):
                for j in range(GB):
                    pool.wait_ge(mb_in[j], (END + k + 1) * 16)
                    gather((END + 1 + k) * GB + j, j, mb_end[:, k, j, :, :])

        def pe_z(pe, n, g, bank, mb_in_sb, chunks):
            if 0 in chunks:
                for j in range(GB):
                    pe.wait_ge(mb_in[j], n * 16 + 16)
            for c in chunks:
                for j in range(GB):
                    tok = g * P + H * j
                    last = pe.matmul(bank[H * j:H * j + H, (g % 2) * 256:(g % 2) * 256 + Z], x1[:, c, tok:tok + H], mb_in_sb[:, j, c, :],
                                     start=(g % 2 == 0 and c == 0), stop=(c == C - 1), tile_position=(0, H * j), skip_group_check=True)
            return last

        def pe_wht(pe, count, p, bank):
            pe.wait_ge(wh_done, count + FREE)
            for i in range(2):
                g = 2 * p + i
                last = pe.transpose(bank[:, g * P:(g + 1) * P], wh[:, i, :], ident)
            last.then_inc(wht_ps, 1)

        def pe_out(pe, c, out_ps, tok, start):
            d = slice(c * P, (c + 1) * P)
            pe.matmul(out_ps, b2_hi[:, d], wht_hi[:, tok], start=start, stop=False, skip_group_check=True)
            pe.matmul(out_ps, b2_hi[:, d], wht_lo[:, tok], start=False, stop=False, skip_group_check=True)
            return pe.matmul(out_ps, b2_lo[:, d], wht_hi[:, tok], start=False, stop=True, skip_group_check=True)

        def pe_layer1(pe, f, m):
            if f in Z_SLOTS:
                g = Z_SLOTS.index(f)
                if g == 0:
                    pe.wait_ge(x1_done, m * C + C)
                    pe.wait_ge(out_ready, m * C + FREE)
                if g == 2:
                    pe.wait_ge(wh_done, m * 2 + (1 + FREE))
                pe_z(pe, m * G + g, g, z_ps, mb, range(C)).then_inc(z_done, 1)
            if f in WHT_SLOTS:
                p = WHT_SLOTS.index(f)
                pe_wht(pe, m * 2 + (p + 1), p, s_ps)
            for c in (c for c in range(C) if OUT_SLOTS[c] == f):
                if c == 0:
                    pe.wait_ge(wht_done, m + 1)
                    pe.wait_ge(whtlo_done, m + 1)
                if c >= 2:
                    pe.wait_ge(out_ready, m * C + (c - 1 + FREE))
                pe_out(pe, c, [z_ps, s_ps][c % 2][:, :], slice(0, TILE), True).then_inc(o_done, 1)

        def pe_end(pe, step, a, k):
            m = NT - 1
            tok = slice(a * HALF, (a + 1) * HALF)
            if step == "down":
                pe_down_half(pe, NT * F - 1, F - 1, a, k).then_inc(end_down, 1)
            if step == "z":
                if k == 0:
                    pe.wait_ge(prod_done, NT * F)
                    pe.wait_ge(silu_done, NT * F)
                pe.wait_ge(x1_done, m * C + 2 * a + k + 1)
                for g in (2 * a, 2 * a + 1):
                    last = pe_z(pe, m * G + g, g, [gate_ps, up_ps][a], mb if g == 0 else mb_end[:, g - 1, :, :, :], (2 * k, 2 * k + 1))
                    if k == 1:
                        last.then_inc(z_done, 1)
            if step == "wht":
                pe.wait_ge(out_ready, m * C + FREE)
                pe_wht(pe, m * 2 + a + 1, a, [s_ps, z_ps][a])
            if step == "out":
                if k == 0:
                    pe.wait_ge(wht_done, m + a + 1)
                    pe.wait_ge(whtlo_done, m + a + 1)
                for i in range(2):
                    last = pe_out(pe, 2 * k + i, end_bank(a, k)[:, i * HALF:(i + 1) * HALF], tok, i == 0)
                last.then_inc(o_done, 1)

        def pe_gate_up(pe, bank, f, k, y_from=None):
            for c in range(C):
                if y_from is not None:
                    pe.wait_ge(yhi_done, y_from + (c + 1))
                    pe.wait_ge(ylo_done, y_from + (c + 1))
                pe.matmul(bank[:, :], w_hi[:, f, k, c, :], y_hi[:, c, :], start=(c == 0), stop=False)
                pe.matmul(bank[:, :], w_hi[:, f, k, c, :], y_lo[:, c, :], start=False, stop=False)
                last = pe.matmul(bank[:, :], w_lo[:, f, k, c, :], y_hi[:, c, :], start=False, stop=(c == C - 1))
            return last

        def pe_down_chunk(pe, f, c, sums, tok, start):
            d = slice(c * P, (c + 1) * P)
            pe.matmul(sums, wd_hi[:, f % 2, d], h_hi[:, f % 2, tok], start=start, stop=False, skip_group_check=True)
            pe.matmul(sums, wd_hi[:, f % 2, d], h_lo[:, f % 2, tok], start=False, stop=False, skip_group_check=True)
            return pe.matmul(sums, wd_lo[:, f % 2, d], h_hi[:, f % 2, tok], start=False, stop=(f == F - 1), skip_group_check=True)

        def pe_down_half(pe, n, f, a, k):
            pe.wait_ge(wdlo_done, n + 1)
            pe.wait_ge(hlo_done, n + 1)
            for i in range(2):
                last = pe_down_chunk(pe, f, 2 * k + i, end_bank(a, k)[:, i * HALF:(i + 1) * HALF], slice(a * HALF, (a + 1) * HALF),
                                     f == 0 and i == 0)
            return last

        def pe_down(pe, n, f, last_tile):
            pe.wait_ge(wdlo_done, n + 1)
            pe.wait_ge(hlo_done, n + 1)
            for i in range(C):
                if last_tile:
                    last = pe_down_half(pe, n, f, i // 2, i % 2)
                else:
                    last = pe_down_chunk(pe, f, i, down_ps[i][:, :], slice(0, TILE), f == 0)
            last.then_inc(down_done, 1)

        def pe_tile(pe, t, first_tile, last_tile=False):
            for f in range(F):
                n = t * F + f
                if first_tile:
                    pe.wait_ge(whi_done, f + 1)
                    pe.wait_ge(wlo_done, f + 1)
                if not (first_tile and f == 0):
                    pe.wait_ge(silu_done, n)
                pe_gate_up(pe, gate_ps, f, 0, t * C if f == 0 else None).then_inc(gate_done, 1)
                if not (first_tile and f == 0):
                    pe.wait_ge(prod_done, n)
                pe_gate_up(pe, up_ps, f, 1).then_inc(up_done, 1)
                if f == 1 and not first_tile:
                    pe.wait_ge(x1_done, t * C)
                if f:
                    pe_down(pe, n - 1, f - 1, last_tile)
                if not first_tile:
                    pe_layer1(pe, f, t - 1)
            if not last_tile:
                pe_down(pe, t * F + (F - 1), F - 1, False)

        @block.tensor
        def _(pe):
            pe.sem_inc(wht_ps, FREE)
            pe.sem_inc(o_done, FREE)

            def aw(e):
                if e >= 2:
                    pe.wait_ge(we_in[e % 4], 16 * (e // 4 + (e % 4 >= 2)))
                if e >= 2:
                    pe.wait_ge(aw_copied, e - 1)
                for ic in range(C):
                    if e == 0:
                        pe.wait_ge(we_part[ic], 16)
                    if e == 1 and ic % 2 == 0:
                        pe.wait_ge(we_half[ic // 2], 16)
                    for oc in range(C):
                        last = pe.matmul(aw_ps[e % 2][ic // 2][:, (ic % 2) * Z:(ic % 2 + 1) * Z], we_sb[:, e % 4, oc, ic * P:(ic + 1) * P],
                                         ra_sb[:, oc, :], start=(oc == 0), stop=(oc == C - 1))
                last.then_inc(aw_done, 1)

            pe.wait_ge(zeros_done, 1)
            for _ in range(IDLE_PRODUCTS):
                pe.matmul(z_ps[:, 0:P], idle_sb[:, :], idle_sb[:, :], start=True, stop=True)
            pe.wait_ge(ra_in, 16)
            for e in range(5):
                aw(e)
            pe.wait_ge(u_done, 1)
            pe.wait_ge(v_done, 2)
            for h in range(H):
                bank = k_ps[h // (H // 2)]
                col = (h % (H // 2)) * NB
                last = pe.matmul(bank[0:NA, col:col + NB], u_tab[:, h, :], v_tab[:, h, :], start=True, stop=True)
            last.then_inc(k_done, 1)
            aw(5)
            aw(6)
            pe.wait_ge(ut_in, 16)
            pe.wait_ge(k_ready, 2)

            def conv(pair, s, peeled):
                pe.wait_ge(toep_in[s], (pair - s) * 4 + 16)
                if not peeled:
                    pe.wait_ge(y_done, pair - 3)
                for k in range(2):
                    for d in range(C):
                        last = pe.matmul(down_ps[s][:, k * C * B + d * B:(k + 1) * C * B], toep[:, s, k, d * P:(d + 1) * P],
                                         uy[:, bass.ds(pair * 2 + k, 1), 0:C - d, :].rearrange("p h c b -> p (h c b)"),
                                         start=(k == 0 and d == 0), stop=(d == C - 1), skip_group_check=True)
                last.then_inc(conv_done, 1)

            for s in range(4):
                conv(s, s, True)
            with pe.Fori(1, PAIRS // 4) as i:
                pe.wait_ge(ut_in, i * 16 + 16)
                for s in range(4):
                    conv(i * 4 + s, s, False)
            aw(7)
            pe_tile(pe, 0, True)
            pe.wait_ge(b2lo_done, 1)
            with pe.Fori(1, NT - 1) as t:
                pe_tile(pe, t, False)
            pe_tile(pe, NT - 1, False, last_tile=True)
            for step, a, k in END_ORDER:
                pe_end(pe, step, a, k)


def kernel(**inputs):
    import numpy as np
    import concourse.bacc as bacc
    from concourse.bass_utils import run_bass_kernel_spmd

    def a(name):
        return np.asarray(inputs[name])

    x = a("x")
    ut = x.reshape(B, H, C, P)[:, :, :, ::-1].transpose(3, 1, 2, 0)

    xt = x.reshape(NT, TILE, C, P).transpose(0, 2, 3, 1).reshape(NT * C, P, TILE)

    def pad(w):
        return np.pad(w, ((0, F * P - D_FF), (0, 0)))

    wgu = np.stack([pad(a(n)).reshape(F, P, C, P).transpose(0, 3, 2, 1) for n in ("L0_ffn_W_gate", "L0_ffn_W_up")], 2)
    wd = pad(a("L0_ffn_W_down").T).reshape(F, P, L).transpose(1, 0, 2)
    we = a("L1_cond_weight").reshape(E, C, P, L).transpose(0, 2, 1, 3)
    ra = np.concatenate([a("L1_ffn_route_w"), a("L1_ffn_A").reshape(ER, L)]).T.reshape(C, P, Z).transpose(1, 0, 2)
    b2 = a("L1_ffn_Bw").transpose(0, 2, 1).reshape(ER, L)
    re, im = a("L0_cond_C")[..., 0].T, a("L0_cond_C")[..., 1].T

    def twice(m):
        return np.concatenate([m, m])

    params = np.stack([np.broadcast_to(a("L0_cond_log_dt"), (P, H)), twice(a("L0_cond_log_A_real").T), twice(a("L0_cond_A_imag").T),
                       np.concatenate([re, im]), np.concatenate([im, re])], 1)
    consts = np.zeros((P, K_END), np.float32)
    consts[:, K_ID:K_ID + P] = np.eye(P)
    consts[:, K_A:K_A + NA] = np.arange(NA)
    consts[:, K_B:K_B + NB] = np.arange(NB)
    consts[:, K_L:K_L + C] = np.arange(L).reshape(C, P).T
    consts[:, K_SIGN] = np.repeat([1, -1], N_STATE)
    consts[:, K_OFF] = np.repeat([0.25, 0.5], N_STATE)
    consts[:, K_RANK:K_RANK + E] = E - np.arange(E)
    arrays = {
        "params": params, "consts": consts, "d_skip": a("L0_cond_D").reshape(1, H),
        "lens": np.broadcast_to(a("itok_B_8_3872"), (P, B)), "ids": a("itok_B_3_7").reshape(1, B),
        "ut": ut, "xt": xt, "wgu": wgu.reshape(F, P, 2 * C * P), "wd": wd, "we": we, "ra": ra, "b2": b2,
    }
    nc = bacc.Bacc("TRN2", target_bir_lowering=False, num_devices=1)
    arrays = {k: np.ascontiguousarray(v) for k, v in arrays.items()}
    aps = {k: nc.dram_tensor(k, v.shape, mybir.dt.from_np(v.dtype), kind="ExternalInput").ap() for k, v in arrays.items()}
    out = nc.dram_tensor("out", (NT * C, P, TILE), F32, kind="ExternalOutput").ap()
    build(nc, out=out, **aps)
    r = run_bass_kernel_spmd(nc, [arrays], core_ids=[0])
    return r.results[0]["out"].reshape(NT, C, P, TILE).transpose(0, 3, 1, 2).reshape(B, H, L)
```
